# Optimizing a Trainium2 kernel written in Bass

```python
import numpy as np
import jax
import jax.numpy as jnp

def _softmax(x, axis=-1):
    return jax.nn.softmax(x, axis=axis)

def _gelu(x):
    return jax.nn.gelu(x, approximate=True)

def _silu(x):
    return jax.nn.silu(x)

def _sigmoid(x):
    return jax.nn.sigmoid(x)

def _layernorm(x, axis=-1, eps=1e-05):
    m = jnp.mean(x, axis=axis, keepdims=True)
    v = jnp.var(x, axis=axis, keepdims=True)
    return (x - m) / jnp.sqrt(v + eps)

def _scatter_add(tgt, idx, src, axis=0):
    return tgt.at[idx].add(src)

def _segment_sum(src, seg, n):
    return jax.ops.segment_sum(src, seg, n)
kernel_name = 'mk_gnn_preln_d2_gnn_r32_e39a25'

def setup_inputs(seed: int=0):
    np.random.seed(seed)
    _w = jnp.asarray

    def _rec_inputs():
        import jax
        import jax.numpy as jnp
        _gk = jax.random.key(seed)
        x = -0.000202 + 1 * jax.random.normal(jax.random.fold_in(_gk, 1), (3125, 128), jnp.float32)
        _s = jax.random.randint(jax.random.fold_in(_gk, 2), (50000,), 0, 3125, jnp.int32)
        _d = jax.random.randint(jax.random.fold_in(_gk, 3), (50000,), 0, 3125, jnp.int32)
        _loop = jnp.arange(3125, dtype=jnp.int32)
        src = jnp.concatenate([_s, _d, _loop])
        dst = jnp.concatenate([_d, _s, _loop])
        _o = jnp.argsort(dst, stable=True)
        src = src[_o]
        dst = dst[_o]
        edge_attr_64 = -5.16925e-05 + 1.00005 * jax.random.normal(jax.random.fold_in(_gk, 11), (103125, 64), jnp.float32)
        return (x, src, dst, edge_attr_64)
    x, src, dst, edge_attr_64 = _rec_inputs()

    def _L0_gnn_setup():
        import jax, jax.numpy as jnp
        import numpy as np
        NEG_SLOPE = 0.2

        def gat_layer(x, src, dst, W, a_src, a_dst, b, n_nodes):
            h = x @ W
            s = h @ a_src
            d = h @ a_dst
            e = jax.nn.leaky_relu(s[src] + d[dst], NEG_SLOPE)
            m = jax.ops.segment_max(e, dst, num_segments=n_nodes)
            m = jnp.where(jnp.isfinite(m), m, 0.0)
            ex = jnp.exp(e - m[dst])
            z = jax.ops.segment_sum(ex, dst, num_segments=n_nodes)
            alpha = ex / z[dst]
            out = jax.ops.segment_sum(alpha[:, None] * h[src], dst, num_segments=n_nodes)
            return out + b
        key = jax.random.key(seed)
        ks = jax.random.split(key, 12)
        N, E, F_IN, F_OUT = (50000, 25000, 128, 128)
        H = 2 * F_OUT
        x = jax.random.normal(ks[0], (N, F_IN), dtype=jnp.float32)
        edge_index = jax.random.randint(ks[1], (2, E), 0, N, dtype=jnp.int64)
        glorot = lambda k, shape: jax.random.uniform(k, shape, jnp.float32, -1.0, 1.0) * jnp.sqrt(6.0 / sum(shape))
        return {'x': x, 'edge_index': edge_index, 'W1': glorot(ks[2], (F_IN, H)), 'a_src1': glorot(ks[3], (H,)) * 0.1, 'a_dst1': glorot(ks[4], (H,)) * 0.1, 'b1': jnp.zeros((H,), jnp.float32), 'W2': glorot(ks[5], (H, F_OUT)), 'a_src2': glorot(ks[6], (F_OUT,)) * 0.1, 'a_dst2': glorot(ks[7], (F_OUT,)) * 0.1, 'b2': jnp.zeros((F_OUT,), jnp.float32)}
    _L0_gnn_all = _L0_gnn_setup()
    _L0_gnn_in = {k: v for k, v in _L0_gnn_all.items() if k in ('W1', 'a_src1', 'a_dst1', 'b1', 'W2', 'a_src2', 'a_dst2', 'b2')}
    del _L0_gnn_all

    def _L1_gnn_setup():
        import jax, jax.numpy as jnp
        import numpy as np
        NEG_SLOPE = 0.2
        key = jax.random.key(seed)
        ks = jax.random.split(key, 10)
        N, E, D, ED = (3125, 50000, 128, 64)
        x = jax.random.normal(ks[0], (N, D), dtype=jnp.float32)
        edge_index = jax.random.randint(ks[1], (2, E), 0, N, dtype=jnp.int32)
        edge_attr = jax.random.normal(ks[2], (E, ED), dtype=jnp.float32)
        s = 1.0 / np.sqrt(D)
        W = jax.random.normal(ks[3], (D, D), dtype=jnp.float32) * s
        att_src = jax.random.normal(ks[4], (D,), dtype=jnp.float32) * s
        att_dst = jax.random.normal(ks[5], (D,), dtype=jnp.float32) * s
        bias = jnp.zeros((D,), dtype=jnp.float32)
        We = jax.random.normal(ks[6], (ED, D), dtype=jnp.float32) / np.sqrt(ED)
        be = jnp.zeros((D,), dtype=jnp.float32)
        return {'x': x, 'edge_index': edge_index, 'edge_attr': edge_attr, 'W': W, 'att_src': att_src, 'att_dst': att_dst, 'bias': bias, 'We': We, 'be': be}
    _L1_gnn_all = _L1_gnn_setup()
    _L1_gnn_in = {k: v for k, v in _L1_gnn_all.items() if k in ('W', 'att_src', 'att_dst', 'bias', 'We', 'be')}
    del _L1_gnn_all
    return {'x': x, 'src': src, 'dst': dst, 'edge_attr_64': edge_attr_64, 'L0_gnn_W1': _L0_gnn_in['W1'], 'L0_gnn_a_src1': _L0_gnn_in['a_src1'], 'L0_gnn_a_dst1': _L0_gnn_in['a_dst1'], 'L0_gnn_b1': _L0_gnn_in['b1'], 'L0_gnn_W2': _L0_gnn_in['W2'], 'L0_gnn_a_src2': _L0_gnn_in['a_src2'], 'L0_gnn_a_dst2': _L0_gnn_in['a_dst2'], 'L0_gnn_b2': _L0_gnn_in['b2'], 'L1_gnn_W': _L1_gnn_in['W'], 'L1_gnn_att_src': _L1_gnn_in['att_src'], 'L1_gnn_att_dst': _L1_gnn_in['att_dst'], 'L1_gnn_bias': _L1_gnn_in['bias'], 'L1_gnn_We': _L1_gnn_in['We'], 'L1_gnn_be': _L1_gnn_in['be']}

def reference(x, src, dst, edge_attr_64, L0_gnn_W1, L0_gnn_a_src1, L0_gnn_a_dst1, L0_gnn_b1, L0_gnn_W2, L0_gnn_a_src2, L0_gnn_a_dst2, L0_gnn_b2, L1_gnn_W, L1_gnn_att_src, L1_gnn_att_dst, L1_gnn_bias, L1_gnn_We, L1_gnn_be):
    import jax
    import jax.numpy as jnp

    def _L0_gnn_ref(x, edge_index, W1, a_src1, a_dst1, b1, W2, a_src2, a_dst2, b2):
        import jax, jax.numpy as jnp
        import numpy as np
        NEG_SLOPE = 0.2

        def gat_layer(x, src, dst, W, a_src, a_dst, b, n_nodes):
            h = x @ W
            s = h @ a_src
            d = h @ a_dst
            e = jax.nn.leaky_relu(s[src] + d[dst], NEG_SLOPE)
            m = jax.ops.segment_max(e, dst, num_segments=n_nodes)
            m = jnp.where(jnp.isfinite(m), m, 0.0)
            ex = jnp.exp(e - m[dst])
            z = jax.ops.segment_sum(ex, dst, num_segments=n_nodes)
            alpha = ex / z[dst]
            out = jax.ops.segment_sum(alpha[:, None] * h[src], dst, num_segments=n_nodes)
            return out + b
        n_nodes = x.shape[0]
        loops = jnp.arange(n_nodes, dtype=edge_index.dtype)
        src = jnp.concatenate([edge_index[0], loops])
        dst = jnp.concatenate([edge_index[1], loops])
        h = gat_layer(x, src, dst, W1, a_src1, a_dst1, b1, n_nodes)
        h = jax.nn.relu(h)
        return gat_layer(h, src, dst, W2, a_src2, a_dst2, b2, n_nodes)

    def _L1_gnn_ref(x, edge_index, edge_attr, W, att_src, att_dst, bias, We, be):
        import jax, jax.numpy as jnp
        import numpy as np
        NEG_SLOPE = 0.2
        N = x.shape[0]
        edge_feat = edge_attr @ We + be
        h = x @ W
        loop = jnp.arange(N, dtype=edge_index.dtype)
        src = jnp.concatenate([edge_index[0], loop])
        dst = jnp.concatenate([edge_index[1], loop])
        a_s = h @ att_src
        a_d = h @ att_dst
        e = jax.nn.leaky_relu(a_s[src] + a_d[dst], NEG_SLOPE)
        seg_max = jax.ops.segment_max(e, dst, num_segments=N)
        e = jnp.exp(e - seg_max[dst])
        denom = jax.ops.segment_sum(e, dst, num_segments=N)
        alpha = e / (denom[dst] + 1e-16)
        out = jax.ops.segment_sum(h[src] * alpha[:, None], dst, num_segments=N)
        return out + bias
    edge_index = jnp.stack([src, dst])
    h = jnp.maximum(_layernorm(x, axis=-1), 0.0)
    x = x + _L0_gnn_ref(h, edge_index, L0_gnn_W1, L0_gnn_a_src1, L0_gnn_a_dst1, L0_gnn_b1, L0_gnn_W2, L0_gnn_a_src2, L0_gnn_a_dst2, L0_gnn_b2)
    h = jnp.maximum(_layernorm(x, axis=-1), 0.0)
    x = x + _L1_gnn_ref(h, edge_index, edge_attr_64, L1_gnn_W, L1_gnn_att_src, L1_gnn_att_dst, L1_gnn_bias, L1_gnn_We, L1_gnn_be)
    return x

_drawn_inputs = setup_inputs


def setup_inputs(seed=0):
    import zlib

    import numpy as np

    out = dict(_drawn_inputs(seed))
    spreads = {'L0_gnn_b1': (0.0, 0.1),
     'L0_gnn_b2': (0.0, 0.1),
     'L1_gnn_bias': (0.0, 0.1),
     'L1_gnn_be': (0.0, 0.1)}
    factors = {'L0_gnn_a_src1': 29.265,
     'L0_gnn_a_dst1': 64.0,
     'L0_gnn_a_src2': 64.0,
     'L0_gnn_a_dst2': 200.0,
     'L1_gnn_att_dst': 52.179}
    for name, (base, spread) in spreads.items():
        noise = np.random.default_rng([zlib.crc32(name.encode()), seed]).standard_normal(out[name].shape)
        drawn = base * np.exp(spread * noise) if base else spread * noise
        out[name] = jnp.asarray(drawn.astype(out[name].dtype))
    for name, factor in factors.items():
        out[name] = (out[name] * factor).astype(out[name].dtype)
    return out
```

```python
from contextlib import ExitStack

import concourse.bass as bass
from concourse import mybir


def gat_stack_kernel(nc, x, edges, W1, a_src1, a_dst1, b1, W2, a_src2, a_dst2, b2,
                     W3, a_src3, a_dst3, b3, out):
    fp32, bf16 = mybir.dt.float32, mybir.dt.bfloat16
    i32, u8 = mybir.dt.int32, mybir.dt.uint8
    ALU, ACT, AX = mybir.AluOpType, mybir.ActivationFunctionType, mybir.AxisListType
    MAX_OVER_PARTITIONS = bass.bass_isa.ReduceOp.max

    N, D = x.shape
    E = edges.shape[0]
    H1 = W1.shape[1]
    KH = H1 // 128
    P = 125
    T = N // P
    WQ = 5
    NW = N // WQ
    WC = T * WQ
    WG = NW // P
    TW = P // WQ
    SLOTS = 256
    REAL = SLOTS - WQ
    KC = SLOTS // 128
    EP = E // P
    SAMPLE = 25
    NS = EP // SAMPLE
    CAP = 254
    CT = 5
    NC = T // CT
    CD = CT * P
    CW = CD // WQ
    RING = 5
    HW = D + 1
    AW = D + 2
    EX = EP + T
    U = 10
    EPS, SLOPE = 1e-5, 0.2
    MAGIC = 12582912.0
    assert T * P == N and NW * WQ == N and WG * P == NW and EP * P == E and NS * SAMPLE == EP
    assert EX % U == 0 and WC == P

    x_v = x.rearrange("(t p) f -> p t f", p=P)
    out_v = out.rearrange("(t p) f -> p t f", p=P)
    rest_d = nc.dram_tensor("count_rest", (P, T, N), fp32).ap()

    ctx = ExitStack()
    with ctx:
        def sb(name, shape, dt=fp32):
            return ctx.enter_context(nc.sbuf_tensor(name, shape, dt))

        def sem(name):
            return ctx.enter_context(nc.semaphore(name))

        C = sb("C", [P, NW * WC], u8)
        C4 = C[:, :].rearrange("p (w t q) -> p w t q", t=T, q=WQ)
        xr = sb("xr", [P, T, D])
        hA = sb("hA", [P, T, HW])
        hB = sb("hB", [128, T * HW])
        hB3 = hB[0:P, :].rearrange("p (t f) -> p t f", f=HW)
        iota_t = hB[:, 0:P * TW * KC // 2].bitcast(bf16).rearrange("p (c n) -> p c n", c=P)
        scratch = sb("scratch", [128, 2 * P * TW * KC])
        edge_sb = sb("edge_sb", [P, EP, 2], i32)
        gathered = sb("gathered", [P, WG, SLOTS * 2], i32)
        gath4 = gathered[:, :, :].rearrange("p g (e c) -> p g e c", c=2)
        key_lo = sb("key_lo", [128, NW, KC], bf16)
        key_col = sb("key_col", [128, NW, KC], bf16)
        ident = sb("ident", [128, 128])
        w1 = sb("w1", [D, H1])
        w1T = sb("w1T", [128, KH, D])
        w1v = sb("w1v", [D, 2])
        w2 = sb("w2", [128, KH, AW])
        w2T = sb("w2T", [D, KH, 128])
        w3 = sb("w3", [D, AW])
        w3T = sb("w3T", [D, D])
        av1 = sb("av1", [128, KH, 2])
        av2 = sb("av2", [D, 2])
        av3 = sb("av3", [D, 2])
        b1c = sb("b1c", [128, KH])
        b2r = sb("b2r", [P, D])
        b3r = sb("b3r", [P, D])
        zeros = sb("zeros", [P, 512], bf16)
        ones_b = sb("ones_b", [P, 1], bf16)
        ones_f = sb("ones_f", [P, P])
        sampled = sb("sampled", [P, NS])
        win_base = sb("win_base", [P, WG])
        start_f = sb("start_f", [P, WG])
        start_i = sb("start_i", [P, WG], i32)
        covered = sb("covered", [P, 1])
        general = sb("general", [1, 1], i32)
        bn6 = sb("bn6", [P, T, 6])
        mv = sb("mv", [P, T, 2])
        bn6c = sb("bn6c", [P, CT, 6])
        mvc = sb("mvc", [P, CT, 2])
        rstd = sb("rstd", [P, T])
        nbias = sb("nbias", [P, T])
        neghalf = sb("neghalf", [P, T])
        ab = [sb(f"ab{L}", [P, T, 2]) for L in range(3)]
        ext = sb("ext", [P, 2])
        extg = sb("extg", [P, 2])
        span = sb("span", [P, 2])
        a_unit = sb("a_unit", [P, T])
        a_leak = sb("a_leak", [P, T])
        b_low = sb("b_low", [P, T])
        mu = sb("mu", [P, CT])
        e_top = sb("e_top", [P, CT])
        m_top = sb("m_top", [P, CT])
        uv = sb("uv", [P, 2, CT])
        rz = sb("rz", [P, CT])
        featT0 = sb("featT0", [D, CT * P])

        sc_b = scratch[:, :].bitcast(bf16)
        win_dst = hA[:, :, :].rearrange("p t f -> p (t f)")[:, 0:NW]
        before = sc_b[0:P, 0:NS * NW].rearrange("p (k w) -> p k w", k=NS)
        NSL = WG * SLOTS

        def slot_plane(i):
            return scratch[0:P, i * NSL:(i + 1) * NSL].rearrange("p (g e) -> p g e", g=WG)

        k_hi, k_lo, k_dl, k_ok, k_in = (slot_plane(i) for i in range(5))
        OH = P * TW * KC
        hot_lo = [sc_b[:, 2 * i * OH:(2 * i + 1) * OH].rearrange("p (c n) -> p c n", c=P) for i in range(2)]
        hot_col = [sc_b[:, (2 * i + 1) * OH:(2 * i + 2) * OH].rearrange("p (c n) -> p c n", c=P) for i in range(2)]
        g_lo, g_col, g_hi, g_dst, g_win, g_shift = (scratch[0:P, i * EX:(i + 1) * EX] for i in range(6))
        g_at = 6 * EX
        g_iota = scratch[0:P, g_at:g_at + WQ * WC]
        g_plane = scratch[0:P, g_at + 640:g_at + 640 + WQ * WC]
        g_hot = scratch[0:P, g_at + 1280:g_at + 1280 + U * 3 * P].bitcast(bf16).rearrange(
            "p (u k c) -> p u k c", u=U, k=6)
        ringA = [scratch[0:P, i * CD:(i + 1) * CD] for i in range(RING)]
        ringB = [scratch[0:P, (RING + i) * CD:(RING + i + 1) * CD] for i in range(RING)]
        at = 2 * RING * CD
        top_a = scratch[0:P, at:at + CD]
        rest_sb = scratch[0:P, at + CD:at + 2 * CD]
        at += 2 * CD
        agg = scratch[0:P, at:at + CT * D].rearrange("p (t f) -> p t f", f=D)
        at += CT * D
        gn = scratch[0:P, at:at + CT * D].rearrange("p (t f) -> p t f", f=D)
        at += CT * D
        featT = scratch[0:D, at:at + CD]
        at += CD
        h1T = scratch[:, at:at + KH * CD].rearrange("p (k n) -> p k n", k=KH)
        assert at + KH * CD <= 2 * OH and g_at + 1280 + U * 3 * P <= 2 * OH and NS * NW <= 4 * OH

        ps = ctx.enter_context(nc.psum_tensor("ps", [128, 8 * 512], fp32))

        def tiles(at, n=CT, width=P, rows=P):
            return ps[0:rows, at:at + 128 * n].rearrange("p (t c) -> p t c", c=128)[:, :, 0:width]

        def acc_at(t):
            return 512 * (t // 3) + HW * (t % 3)

        ROWU, ROWV, WORK = 1024, 1024 + 128 * CT, 2560

        def new_at(t):
            return WORK + 512 * (t // 3) + AW * (t % 3)

        acc3 = [ps[0:P, 0:3 * HW].rearrange("p (t f) -> p t f", f=HW),
                ps[0:P, 512:512 + 2 * HW].rearrange("p (t f) -> p t f", f=HW)]
        new3 = [ps[0:P, WORK:WORK + 3 * AW].rearrange("p (t f) -> p t f", f=AW),
                ps[0:P, WORK + 512:WORK + 512 + 2 * AW].rearrange("p (t f) -> p t f", f=AW)]
        PREP, VEC, AB0, CNT, COV = 2560, 2048, 3200, 3584, 3648
        HALF = [(0, (TW + 1) // 2, 0), ((TW + 1) // 2, TW, 2048)]

        edges_in = sem("edges_in")
        x_in = sem("x_in")
        weights_in = sem("weights_in")
        consts = sem("consts")
        dve_consts = sem("dve_consts")
        samples_ok = sem("samples_ok")
        before_ok = sem("before_ok")
        before_sum = sem("before_sum")
        start_lin = sem("start_lin")
        starts_ok = sem("starts_ok")
        gather_in = sem("gather_in")
        keys_lin = sem("keys_lin")
        keys_ok = sem("keys_ok")
        covered_sum = sem("covered_sum")
        flag_ok = sem("flag_ok")
        keys_T = sem("keys_T")
        keys_sb = sem("keys_sb")
        prep_T = sem("prep_T")
        prep_sb = sem("prep_sb")
        prep_v = sem("prep_v")
        prep_done = sem("prep_done")
        hots_ok = sem("hots_ok")
        half_ok = [sem("half0_ok"), sem("half1_ok")]
        half_out = [sem("half0_out"), sem("half1_out")]
        ones_col = sem("ones_col")
        gen_lin = sem("gen_lin")
        gen_hots = sem("gen_hots")
        gen_zero = sem("gen_zero")
        gen_mm = sem("gen_mm")
        gen_out = sem("gen_out")
        gen_plane = sem("gen_plane")
        gen_stored = sem("gen_stored")
        counts_done = sem("counts_done")
        ln_lin = sem("ln_lin")
        ln_stats = sem("ln_stats")
        ln_pool = sem("ln_pool")
        ln_ready = sem("ln_ready")
        g0_ready = sem("g0_ready")
        g0_T = sem("g0_T")
        g0_sb = sem("g0_sb")
        ab0_ps = sem("ab0_ps")
        ab_ready = sem("ab_ready")
        ext_lin = sem("ext_lin")
        ext_ready = sem("ext_ready")
        extg_ready = sem("extg_ready")
        scal_lin = sem("scal_lin")
        scal_ready = sem("scal_ready")
        e_ready = sem("e_ready")
        mx_done = sem("mx_done")
        p_ready = sem("p_ready")
        pe_done = sem("pe_done")
        top_done = sem("top_done")
        top_T = sem("top_T")
        top_max = sem("top_max")
        m_lin = sem("m_lin")
        uv_ready = sem("uv_ready")
        rows_ready = sem("rows_ready")
        rz_ready = sem("rz_ready")
        agg_ready = sem("agg_ready")
        feat_T = sem("feat_T")
        feat_sb = sem("feat_sb")
        h1_ps = sem("h1_ps")
        h1_sb = sem("h1_sb")
        new_ps = sem("new_ps")
        new_sb = sem("new_sb")
        res_lin = sem("res_lin")
        x2_ready = sem("x2_ready")
        g_ready = sem("g_ready")
        y_ready = sem("y_ready")
        out_done = sem("out_done")
        rest_in = sem("rest_in")
        rest_e = sem("rest_e")
        rest_mx = sem("rest_mx")
        rest_p = sem("rest_p")
        rest_pe = sem("rest_pe")

        N_WEIGHTS, N_CONSTS = 15, 7
        LAYERS = 3
        h_of = [hA[:, :, :], hB3, hA[:, :, :]]
        new_of = [hB3, hA[:, :, :], None]

        def step_no(L, c, s):
            return (L * NC + c) * T + s

        block = ctx.enter_context(nc.Block())

        @block.sync
        def _(sp):
            sp.dma_start(edge_sb[:, :, :], edges.rearrange("(p k) c -> p k c", p=P)).then_inc(edges_in, 16)
            sp.dma_start(xr[:, :, :], x_v).then_inc(x_in, 16)
            sp.dma_start(w1[:, :], W1).then_inc(weights_in, 16)
            sp.dma_start(w2[:, :, 0:D], W2.rearrange("(k p) f -> p k f", p=128)).then_inc(weights_in, 16)
            sp.dma_start(w3[:, 0:D], W3).then_inc(weights_in, 16)
            for k in range(KH):
                sp.dma_start(b1c[:, k:k + 1], b1[128 * k:128 * (k + 1)].unsqueeze(1)).then_inc(weights_in, 16)
            for i, a in enumerate((a_src1, a_dst1)):
                for k in range(KH):
                    sp.dma_start(av1[:, k, i:i + 1], a[128 * k:128 * (k + 1)].unsqueeze(1)).then_inc(weights_in, 16)
            for v, pair in ((av2, (a_src2, a_dst2)), (av3, (a_src3, a_dst3))):
                for i, a in enumerate(pair):
                    sp.dma_start(v[:, i:i + 1], a.unsqueeze(1)).then_inc(weights_in, 16)
            sp.dma_start(b2r[:, :], b2.unsqueeze(0).broadcast_to([P, D])).then_inc(weights_in, 16)
            sp.dma_start(b3r[:, :], b3.unsqueeze(0).broadcast_to([P, D])).then_inc(weights_in, 16)

            sp.wait_ge(flag_ok, 1)
            with sp.If(sp.value_load(general[0:1, 0:1], min_val=0, max_val=1)):
                with sp.Fori(0, P) as b:
                    first = sp.snap(b * WQ * WQ)
                    sp.wait_ge(gen_plane, b + 1)
                    sp.dma_start(rest_d[:, :, bass.ds(first, WQ * WQ)],
                                 g_plane.rearrange("p (t d) -> p t d", t=T)).then_inc(gen_stored, 16)

            def rest_loads(L, c):
                with sp.If(sp.value_load(general[0:1, 0:1], min_val=0, max_val=1)):
                    sp.wait_ge(gen_stored, 16 * P)
                    with sp.Fori(0, T) as s:
                        tile, first = sp.snap(s + 0), sp.snap(c * CD)
                        sp.wait_ge(rest_pe, step_no(L, c, s))
                        sp.wait_ge(counts_done, 1)
                        sp.dma_start(rest_sb, rest_d[:, bass.ds(tile, 1), bass.ds(first, CD)].rearrange(
                            "p t d -> p (t d)")).then_inc(rest_in, 16)

            def store(c):
                sp.wait_ge(y_ready, c + 1)
                sp.dma_start(out_v[:, bass.ds(c * CT, CT), :], xr[:, bass.ds(c * CT, CT), :]).then_inc(out_done, 16)

            for L in range(LAYERS - 1):
                with sp.Fori(0, NC) as c:
                    rest_loads(L, c)
            for c in range(NC):
                if c:
                    store(c - 1)
                rest_loads(LAYERS - 1, c)
            store(NC - 1)
            sp.wait_ge(out_done, 16 * NC)

        @block.gpsimd
        def _(pool):
            g = nc.gpsimd
            g.iota(win_dst, [[WQ, NW]], 0, channel_multiplier=0,
                   allow_small_or_imprecise_dtypes=True).then_inc(consts, 1)
            g.iota(win_base[:, :], [[WQ * P, WG]], 0, channel_multiplier=WQ,
                   allow_small_or_imprecise_dtypes=True).then_inc(consts, 1)
            g.iota(gath4[:, :, REAL:SLOTS, :], [[WQ * P, WG], [1, WQ], [0, 2]], 0,
                   channel_multiplier=WQ).then_inc(consts, 1)
            g.memset(ident[:, :], 1.0).then_inc(consts, 1)
            pool.wait_ge(consts, 4)
            g.affine_select(out=ident[:, :], in_=ident[:, :], compare_op=ALU.is_equal, fill=0.0, base=0,
                            pattern=[[-1, 128]], channel_multiplier=1).then_inc(consts, 1)
            g.iota(iota_t, [[1, P], [0, TW * KC]], 0, channel_multiplier=0,
                   allow_small_or_imprecise_dtypes=True).then_inc(consts, 1)
            g.memset(neghalf[:, :], -0.5).then_inc(consts, 1)
            pool.wait_ge(consts, N_CONSTS)
            pool.wait_ge(starts_ok, 1)
            for i in range(WG):
                g.indirect_dma_start(gathered[:, i, 0:2 * REAL], None, edges,
                                     bass.IndirectOffsetOnAxis(ap=start_i[:, i:i + 1], axis=0)
                                     ).then_inc(gather_in, 16)

            def norm_scalars(var, mean, r, nb, half, n):
                g.tensor_scalar(r, var, EPS, None, ALU.add).then_inc(ln_pool, 1)
                pool.wait_ge(ln_pool, n + 1)
                g.tensor_tensor(r, r, half, ALU.pow).then_inc(ln_pool, 1)
                g.tensor_scalar(nb, mean, -1.0, None, ALU.mult).then_inc(ln_pool, 1)
                pool.wait_ge(ln_pool, n + 3)
                g.tensor_tensor(nb, nb, r, ALU.mult).then_inc(ln_ready, 1)

            pool.wait_ge(ln_stats, 1)
            norm_scalars(mv[:, :, 1], mv[:, :, 0], rstd[:, :], nbias[:, :], neghalf[:, :], 0)
            pool.wait_ge(hots_ok, T)
            g.memset(hB3[:, :, D:HW], 1.0).then_inc(ones_col, 1)

            def extremes(L):
                pool.wait_ge(ext_ready, L + 1)
                g.partition_all_reduce(extg[:, :], ext[:, :], P, MAX_OVER_PARTITIONS).then_inc(extg_ready, 1)

            def residual(c):
                xc = xr[:, c * CT:(c + 1) * CT, :]
                pool.wait_ge(agg_ready, NC + c + 1)
                g.tensor_tensor(xc, xc, agg, ALU.add).then_inc(res_lin, 1)
                pool.wait_ge(res_lin, c + 1)
                g.tensor_tensor(xc, xc, b2r[:, :].unsqueeze(1).broadcast_to([P, CT, D]),
                                ALU.add).then_inc(x2_ready, 1)
                pool.wait_ge(ln_stats, c + 2)
                pool.wait_ge(g_ready, c)
                norm_scalars(mvc[:, :, 1], mvc[:, :, 0], rstd[:, 0:CT], nbias[:, 0:CT], neghalf[:, 0:CT],
                             c * 3 + 3)

            def result(c):
                xc = xr[:, c * CT:(c + 1) * CT, :]
                pool.wait_ge(agg_ready, 2 * NC + c + 1)
                g.tensor_tensor(xc, xc, agg, ALU.add).then_inc(res_lin, 1)
                pool.wait_ge(res_lin, c + NC + 1)
                g.tensor_tensor(xc, xc, b3r[:, :].unsqueeze(1).broadcast_to([P, CT, D]),
                                ALU.add).then_inc(y_ready, 1)

            pool.wait_ge(weights_in, 16 * N_WEIGHTS)
            extremes(0)
            extremes(1)
            for c in range(NC):
                residual(c)
            extremes(2)
            for c in range(NC):
                result(c)

        @block.vector
        def _(dve):
            v = nc.vector
            v.memset(ones_b[:, :], 1.0)
            v.memset(ones_f[:, :], 1.0)
            v.memset(zeros[:, :], 0.0).then_inc(dve_consts, 1)
            dve.wait_ge(edges_in, 16)
            v.tensor_copy(sampled[:, :], edge_sb[:, :, :].rearrange("p (k r) c -> p k r c", r=SAMPLE)[:, :, 0, 1]
                          ).then_inc(samples_ok, 1)
            dve.wait_ge(samples_ok, 1)
            dve.wait_ge(consts, N_CONSTS)
            for k in range(NS):
                v.tensor_scalar(before[:, k, :], win_dst, sampled[:, k:k + 1], None,
                                ALU.is_gt).then_inc(before_ok, 1)
            dve.wait_ge(before_sum, 1)
            v.tensor_scalar(start_f[:, :], ps[0:P, CNT:CNT + WG], float(SAMPLE), float(1 - SAMPLE),
                            ALU.mult, ALU.add).then_inc(start_lin, 1)
            dve.wait_ge(start_lin, 1)
            v.tensor_scalar(start_i[:, :], start_f[:, :], 0.0, float(E - REAL), ALU.max,
                            ALU.min).then_inc(starts_ok, 1)
            dve.wait_ge(x_in, 16)
            for t in range(T):
                last = v.bn_stats(bn6[:, t, :], xr[:, t, :])
            last.then_inc(ln_lin, 1)
            dve.wait_ge(ln_lin, 1)
            for t in range(T):
                last = v.bn_aggr(mv[:, t, :], bn6[:, t, :])
            last.then_inc(ln_stats, 1)
            v.memset(hA[:, :, D:HW], 1.0).then_inc(dve_consts, 1)
            dve.wait_ge(gather_in, 16 * WG)
            src, dst = gath4[:, :, :, 0], gath4[:, :, :, 1]
            v.tensor_scalar(k_hi, src, 1.0 / P, -0.5 + 0.5 / P, ALU.mult, ALU.add).then_inc(keys_lin, 1)
            v.tensor_tensor(k_dl, dst, win_base[:, :].unsqueeze(2).broadcast_to([P, WG, SLOTS]),
                            ALU.subtract).then_inc(keys_lin, 1)
            dve.wait_ge(keys_lin, 1)
            v.tensor_scalar(k_hi, k_hi, MAGIC, MAGIC, ALU.add, ALU.subtract).then_inc(keys_lin, 1)
            dve.wait_ge(keys_lin, 2)
            v.tensor_scalar(k_in, k_dl, 0.0, None, ALU.is_ge).then_inc(keys_lin, 1)
            dve.wait_ge(keys_lin, 3)
            v.scalar_tensor_tensor(k_lo, k_hi, -float(P), src, ALU.mult, ALU.add).then_inc(keys_lin, 1)
            dve.wait_ge(keys_lin, 4)
            v.scalar_tensor_tensor(k_ok, k_dl, float(WQ - 1), k_in, ALU.is_le, ALU.mult).then_inc(keys_lin, 1)
            v.scalar_tensor_tensor(k_hi, k_hi, float(WQ), k_dl, ALU.mult, ALU.add).then_inc(keys_lin, 1)
            dve.wait_ge(keys_lin, 7)
            v.scalar_tensor_tensor(k_hi, k_hi, 1.0, k_ok, ALU.add, ALU.mult).then_inc(keys_ok, 1)
            v.tensor_reduce(covered[:, :], k_ok, AX.XY, ALU.add).then_inc(keys_ok, 1)
            dve.wait_ge(covered_sum, 1)
            v.tensor_scalar(general[0:1, 0:1], ps[0:1, COV:COV + 1], float(E + N), None,
                            ALU.not_equal).then_inc(flag_ok, 1)
            dve.wait_ge(keys_sb, 1)

            def one_hots(t, i, behind):
                if behind:
                    dve.wait_ge(half_ok[1], t - 1)
                for hot, key in ((hot_lo[i], key_lo), (hot_col[i], key_col)):
                    keys = key[:, bass.ds(t * TW, TW), :].rearrange("p w k -> p (w k)")
                    last = v.tensor_tensor(hot, keys.unsqueeze(1).broadcast_to([128, P, TW * KC]), iota_t,
                                           ALU.is_equal)
                last.then_inc(hots_ok, 1)

            one_hots(0, 0, False)
            one_hots(1, 1, False)
            with dve.Fori(2, T - 1, 2) as t:
                one_hots(t, 0, True)
                one_hots(t + 1, 1, True)
            one_hots(T - 1, 0, True)
            dve.wait_ge(half_out[0], T)
            dve.wait_ge(half_out[1], T)

            dve.wait_ge(flag_ok, 1)
            with dve.If(dve.value_load(general[0:1, 0:1], min_val=0, max_val=1)):
                n = [0]

                def then(ins):
                    n[0] += 1
                    ins.then_inc(gen_lin, 1)
                    dve.wait_ge(gen_lin, n[0])

                then(v.memset(g_win, 0.0))
                then(v.tensor_copy(g_lo[:, 0:EP], edge_sb[:, :, 0]))
                then(v.tensor_copy(g_dst[:, 0:EP], edge_sb[:, :, 1]))
                for t in range(T):
                    then(v.tensor_scalar(g_lo[:, EP + t:EP + t + 1], win_base[:, 0:1], 1.0 / WQ, float(P * t),
                                         ALU.mult, ALU.add))
                then(v.tensor_scalar(g_lo[:, EP:EX], g_lo[:, EP:EX], MAGIC, MAGIC, ALU.add, ALU.subtract))
                then(v.tensor_copy(g_dst[:, EP:EX], g_lo[:, EP:EX]))
                then(v.tensor_scalar(g_hi, g_lo, 1.0 / P, -0.5 + 0.5 / P, ALU.mult, ALU.add))
                then(v.tensor_scalar(g_hi, g_hi, MAGIC, MAGIC, ALU.add, ALU.subtract))
                then(v.scalar_tensor_tensor(g_lo, g_hi, -float(P), g_lo, ALU.mult, ALU.add))
                then(v.tensor_scalar(g_win, g_dst, 1.0 / WQ, -0.5 + 0.5 / WQ, ALU.mult, ALU.add))
                then(v.tensor_scalar(g_win, g_win, MAGIC, MAGIC, ALU.add, ALU.subtract))
                then(v.scalar_tensor_tensor(g_col, g_hi, float(WQ), g_dst, ALU.mult, ALU.add))
                then(v.scalar_tensor_tensor(g_col, g_win, float(WC - WQ), g_col, ALU.mult, ALU.add))
                for w in range(WQ):
                    then(v.tensor_copy(g_iota[:, WC * w:WC * (w + 1)], win_dst[:, 0:WC]))
                    then(v.tensor_scalar(g_iota[:, WC * w:WC * (w + 1)], g_iota[:, WC * w:WC * (w + 1)],
                                         1.0 / WQ, float(WC * w), ALU.mult, ALU.add))
                then(v.tensor_scalar(g_iota, g_iota, MAGIC, MAGIC, ALU.add, ALU.subtract))
                then(v.tensor_copy(g_shift, g_col))
                HAND = EX // U
                with dve.Fori(0, P) as b:
                    with dve.Fori(0, HAND) as i:
                        dve.wait_ge(gen_mm, b * HAND + i)
                        for u in range(U):
                            e = bass.ds(i * U + u, 1)
                            v.tensor_scalar(g_hot[:, u, 0, :], g_iota[:, 0:P], g_lo[:, e], None, ALU.is_equal)
                            last = v.tensor_scalar(g_hot[:, u, 1:6, :].rearrange("p k c -> p (k c)"), g_iota,
                                                   g_shift[:, e], None, ALU.is_equal)
                        last.then_inc(gen_hots, 1)
                    dve.wait_ge(gen_mm, b * HAND + HAND)
                    v.tensor_scalar(C[:, bass.ds(b * WQ * WC, WQ * WC)].rearrange("p (w c) -> p w c", w=WQ),
                                    tiles(0, WQ), float(CAP), None, ALU.min)
                    dve.wait_ge(gen_stored, b * 16)
                    for w in range(WQ):
                        last = v.tensor_scalar(
                            g_plane.rearrange("p (t w q) -> p t w q", t=T, w=WQ)[:, :, w, :],
                            ps[0:P, 128 * w:128 * w + WC].rearrange("p (t q) -> p t q", q=WQ),
                            float(CAP), float(CAP), ALU.max, ALU.subtract)
                    last.then_inc(gen_plane, 1)
                    v.tensor_scalar(g_shift, g_shift, -float(WQ * WC), None, ALU.add).then_inc(gen_out, 1)
                    dve.wait_ge(gen_out, b + 1)
                dve.wait_ge(gen_stored, 16 * P)
            v.memset(rz[:, :], 0.0).then_inc(counts_done, 1)

            def scalars(L):
                a, b = ab[L][:, :, 0], ab[L][:, :, 1]
                dve.wait_ge(ab_ready, L + 1)
                v.tensor_reduce(ext[:, 0:1], a, AX.X, ALU.max).then_inc(ext_lin, 1)
                v.tensor_scalar(a_leak[:, :], a, -1.0, None, ALU.mult).then_inc(ext_lin, 1)
                dve.wait_ge(ext_lin, 3 * L + 2)
                v.tensor_reduce(ext[:, 1:2], a_leak[:, :], AX.X, ALU.max).then_inc(ext_ready, 1)
                dve.wait_ge(ext_ready, L + 1)
                v.tensor_scalar(a_leak[:, :], a, SLOPE, None, ALU.mult).then_inc(ext_lin, 1)
                dve.wait_ge(extg_ready, L + 1)
                v.tensor_tensor(span[:, 0:1], extg[:, 0:1], extg[:, 1:2], ALU.add).then_inc(scal_lin, 1)
                v.tensor_scalar(b_low[:, :], b, extg[:, 1:2], None, ALU.subtract).then_inc(scal_lin, 1)
                dve.wait_ge(scal_lin, 4 * L + 1)
                v.tensor_scalar(span[:, 0:1], span[:, 0:1], 1e-30, None, ALU.max).then_inc(scal_lin, 1)
                dve.wait_ge(scal_lin, 4 * L + 3)
                v.reciprocal(span[:, 1:2], span[:, 0:1]).then_inc(scal_lin, 1)
                dve.wait_ge(scal_lin, 4 * L + 4)
                v.tensor_scalar(a_unit[:, :], a, extg[:, 1:2], span[:, 1:2], ALU.add,
                                ALU.mult).then_inc(scal_ready, 1)
                dve.wait_ge(scal_ready, L + 1)

            def top_step(L, c, s):
                counts = C4[:, bass.ds(c * CW, CW), s, :]
                top = top_a.rearrange("p (w q) -> p w q", q=WQ)
                if s == 0:
                    if not (L == 0 and isinstance(c, int) and c == 0):
                        dve.wait_ge(top_T, L * NC + c)
                    v.tensor_scalar(top, counts, a_unit[:, 0:1], None, ALU.min).then_inc(top_done, 1)
                else:
                    dve.wait_ge(top_done, step_no(L, c, s))
                    v.scalar_tensor_tensor(top, counts, a_unit[:, s:s + 1], top, ALU.min,
                                           ALU.max).then_inc(top_done, 1)

            def top_rows(L, c, first):
                n = L * NC + c
                tc = bass.ds(c * CT, CT)
                dve.wait_ge(top_T, n + 1)
                v.tensor_reduce(mu[:, :], tiles(WORK), AX.X, ALU.max).then_inc(top_max, 1)
                dve.wait_ge(top_max, n + 1)
                v.scalar_tensor_tensor(e_top[:, :], mu[:, :], span[:, 0:1], b_low[:, tc], ALU.mult,
                                       ALU.add).then_inc(m_lin, 1)
                dve.wait_ge(m_lin, 2 * n + 1)
                v.scalar_tensor_tensor(m_top[:, :], e_top[:, :], SLOPE, e_top[:, :], ALU.mult,
                                       ALU.max).then_inc(m_lin, 1)
                if not (L == 0 and first):
                    dve.wait_ge(rows_ready, n)
                dve.wait_ge(m_lin, 2 * n + 2)
                v.tensor_tensor(uv[:, 0, :], ab[L][:, tc, 1], m_top[:, :], ALU.subtract)
                v.scalar_tensor_tensor(uv[:, 1, :], ab[L][:, tc, 1], SLOPE, m_top[:, :], ALU.mult,
                                       ALU.subtract).then_inc(uv_ready, 1)

            def sums_inverse(L, c, first):
                dve.wait_ge(pe_done, step_no(L, c, T))
                if not (L == 0 and first):
                    dve.wait_ge(agg_ready, L * NC + c)
                v.reciprocal(rz[:, 0:3], acc3[0][:, :, D])
                v.reciprocal(rz[:, 3:CT], acc3[1][:, :, D]).then_inc(rz_ready, 1)

            def statistics(c):
                dve.wait_ge(x2_ready, c + 1)
                dve.wait_ge(ln_ready, c + 1)
                for t in range(CT):
                    last = v.bn_stats(bn6c[:, t, :], xr[:, bass.ds(c * CT + t, 1), :].rearrange("p o f -> p (o f)"))
                last.then_inc(ln_lin, 1)

            def aggregate():
                for t in range(CT):
                    last = v.bn_aggr(mvc[:, t, :], bn6c[:, t, :])
                last.then_inc(ln_stats, 1)

            def rest_steps(L, c):
                with dve.If(dve.value_load(general[0:1, 0:1], min_val=0, max_val=1)):
                    with dve.Fori(0, T) as s:
                        dve.wait_ge(rest_e, step_no(L, c, s) + 1)
                        v.tensor_tensor(ringB[0], ringA[0], ringB[0], ALU.max).then_inc(rest_mx, 1)
                        dve.wait_ge(rest_mx, step_no(L, c, s) + 1)
                        dve.wait_ge(rest_in, 16 * (step_no(L, c, s) + 1))
                        v.scalar_tensor_tensor(ringA[0], ringB[0], 2.0, rest_sb, ALU.min,
                                               ALU.mult).then_inc(rest_p, 1)

            def chunk(L, c, first, last_chunk):
                for s in range(T):
                    n = step_no(L, c, s)
                    A, B = ringA[s % RING], ringB[s % RING]
                    if not first and s == 5 and L == 1:
                        dve.wait_ge(ln_lin, c + 1)
                    dve.wait_ge(e_ready, n + 1)
                    v.tensor_tensor(B, A, B, ALU.max).then_inc(mx_done, 1)
                    if not last_chunk and 2 * s < T:
                        top_step(L, c + 1, 2 * s)
                    dve.wait_ge(mx_done, n + 1)
                    v.scalar_tensor_tensor(A.rearrange("p (w q) -> p w q", q=WQ),
                                           B.rearrange("p (w q) -> p w q", q=WQ), 2.0,
                                           C4[:, bass.ds(c * CW, CW), s, :], ALU.min,
                                           ALU.mult).then_inc(p_ready, 1)
                    if not last_chunk and 2 * s + 1 < T:
                        top_step(L, c + 1, 2 * s + 1)
                    if not first and s == 1:
                        sums_inverse(L, c - 1, False)
                    if not first and s == 4 and L == 1:
                        statistics(c - 1)
                    if not first and s == 5 and L == 1:
                        aggregate()
                    if s == 4:
                        rest_steps(L, c)
                    if not last_chunk and s == 19:
                        top_rows(L, c + 1, False)

            for L in range(LAYERS):
                scalars(L)
                for s in range(T):
                    top_step(L, 0, s)
                top_rows(L, 0, True)
                chunk(L, 0, True, False)
                with dve.Fori(1, NC - 1) as c:
                    chunk(L, c, False, False)
                chunk(L, NC - 1, False, True)
                sums_inverse(L, NC - 1, False)
                if L == 1:
                    statistics(NC - 1)
                    dve.wait_ge(ln_lin, NC + 1)
                    aggregate()

        @block.scalar
        def _(act):
            a_ = nc.scalar
            act.wait_ge(prep_T, 1)
            a_.activation(w1T[:, :, :], ps[:, PREP:PREP + KH * 128].rearrange("p (k f) -> p k f", k=KH), ACT.Copy)
            a_.activation(w2T[:, :, :], ps[:, PREP + 256:PREP + 512].rearrange("p (k f) -> p k f", k=KH), ACT.Copy)
            a_.activation(w3T[:, :], ps[:, PREP + 512:PREP + 640], ACT.Copy).then_inc(prep_sb, 1)
            act.wait_ge(prep_v, 1)
            a_.activation(w1v[:, :], ps[:, VEC:VEC + 2], ACT.Copy)
            for k in range(KH):
                a_.activation(w2[:, k, D:AW], ps[:, VEC + 2 + 2 * k:VEC + 4 + 2 * k], ACT.Copy)
            a_.activation(w3[:, D:AW], ps[:, VEC + 6:VEC + 8], ACT.Copy).then_inc(prep_done, 1)
            act.wait_ge(before_sum, 1)
            act.wait_ge(ln_ready, 1)
            for t in range(T):
                last = a_.activation(hA[:, t, 0:D], xr[:, t, :], ACT.Relu, bias=nbias[:, t:t + 1],
                                     scale=rstd[:, t:t + 1])
            last.then_inc(g0_ready, 1)
            for c in range(NC):
                act.wait_ge(g0_T, c + 1)
                if c:
                    act.wait_ge(ab0_ps, c)
                a_.activation(featT0[:, :].rearrange("p (t n) -> p t n", n=P), tiles(0, rows=D),
                              ACT.Copy).then_inc(g0_sb, 1)
            act.wait_ge(ab0_ps, NC)
            a_.activation(ab[0][:, :, :], ps[0:P, AB0:AB0 + 2 * T].rearrange("p (t i) -> p t i", i=2),
                          ACT.Copy).then_inc(ab_ready, 1)
            act.wait_ge(keys_T, 1)
            for k in range(KC):
                a_.activation(key_lo[:, :, k].rearrange("p (g w) -> p g w", g=WG),
                              tiles(128 * WG * k, WG, rows=128), ACT.Copy)
            for k in range(KC):
                last = a_.activation(key_col[:, :, k].rearrange("p (g w) -> p g w", g=WG),
                                     tiles(128 * WG * (KC + k), WG, rows=128), ACT.Copy, bias=-1.0)
            last.then_inc(keys_sb, 1)
            with act.Fori(0, T) as t:
                for i, (w0, w1_, at_) in enumerate(HALF):
                    act.wait_ge(half_ok[i], t + 1)
                    a_.activation(C[:, bass.ds((t * TW + w0) * WC, (w1_ - w0) * WC)].rearrange(
                        "p (w c) -> p w c", c=WC), tiles(at_, w1_ - w0), ACT.Copy).then_inc(half_out[i], 1)

            def exps(A, B, a, al, out_sem):
                a_.activation(A.rearrange("p (t n) -> p t n", n=P), tiles(ROWU), ACT.Exp, bias=a)
                a_.activation(B.rearrange("p (t n) -> p t n", n=P), tiles(ROWV), ACT.Exp,
                              bias=al).then_inc(out_sem, 1)

            def rest_steps(L, c):
                act.wait_ge(flag_ok, 1)
                with act.If(act.value_load(general[0:1, 0:1], min_val=0, max_val=1)):
                    act.wait_ge(pe_done, step_no(L, c, RING))
                    with act.Fori(0, T) as s:
                        act.wait_ge(rest_pe, step_no(L, c, s))
                        one = bass.ds(s, 1)
                        exps(ringA[0], ringB[0], ab[L][:, one, 0], a_leak[:, one], rest_e)

            def scale_sums(L, c):
                n = L * NC + c
                act.wait_ge(rz_ready, n + 1)
                if L == 0:
                    act.wait_ge(feat_T, c)
                elif L == 1:
                    act.wait_ge(x2_ready, c)
                else:
                    act.wait_ge(y_ready, c)
                for t in range(CT):
                    last = a_.activation(agg[:, t, :], ps[0:P, acc_at(t):acc_at(t) + D], ACT.Copy,
                                         scale=rz[:, t:t + 1])
                last.then_inc(agg_ready, 1)

            def copy_featT(L, c):
                act.wait_ge(feat_T, L * NC + c + 1)
                a_.activation(featT.rearrange("p (t n) -> p t n", n=P), tiles(WORK, rows=D),
                              ACT.Copy).then_inc(feat_sb, 1)

            def hidden(c):
                act.wait_ge(h1_ps, c + 1)
                for k in range(KH):
                    last = a_.activation(h1T[:, k, :].rearrange("p (t n) -> p t n", n=P),
                                         tiles(WORK + 128 * CT * k, rows=128), ACT.Relu, bias=b1c[:, k:k + 1])
                last.then_inc(h1_sb, 1)

            def new_features(L, c):
                act.wait_ge(new_ps, L * NC + c + 1)
                if L == 0:
                    act.wait_ge(ones_col, 1)
                for i, (t0, t1) in enumerate(((0, 3), (3, CT))):
                    tc = bass.ds(c * CT + t0, t1 - t0)
                    a_.activation(new_of[L][:, tc, 0:D], new3[i][:, :, 0:D], ACT.Copy)
                    last = a_.activation(ab[L + 1][:, tc, :], new3[i][:, :, D:AW], ACT.Copy)
                last.then_inc(new_sb, 1)

            def normalise(c):
                act.wait_ge(ln_ready, c + 2)
                act.wait_ge(feat_T, NC + c)
                for t in range(CT):
                    one = bass.ds(c * CT + t, 1)
                    last = a_.activation(gn[:, t, :], xr[:, one, :].rearrange("p o f -> p (o f)"), ACT.Relu,
                                         bias=nbias[:, t:t + 1], scale=rstd[:, t:t + 1])
                last.then_inc(g_ready, 1)

            def chunk(L, c, first):
                for s in range(T):
                    if s == 0:
                        act.wait_ge(rows_ready, L * NC + c + 1)
                        if first:
                            act.wait_ge(scal_ready, L + 1)
                            if L == 0:
                                act.wait_ge(counts_done, 1)
                    if not (L == 0 and first and s < RING):
                        act.wait_ge(pe_done, step_no(L, c, s) - (RING - 1))
                    exps(ringA[s % RING], ringB[s % RING], ab[L][:, s, 0:1], a_leak[:, s:s + 1], e_ready)
                    if not first:
                        if s == 3:
                            scale_sums(L, c - 1)
                        if L == 0 and s == 5:
                            copy_featT(L, c - 1)
                        if L == 0 and s == 8:
                            hidden(c - 1)
                        if L == 0 and s == 11:
                            new_features(L, c - 1)
                        if L == 1 and s == 9:
                            normalise(c - 1)
                        if L == 1 and s == 13:
                            copy_featT(L, c - 1)
                        if L == 1 and s == 17:
                            new_features(L, c - 1)
                    if s == 4:
                        rest_steps(L, c)

            for L in range(LAYERS):
                chunk(L, 0, True)
                with act.Fori(1, NC) as c:
                    chunk(L, c, False)
                scale_sums(L, NC - 1)
                if L == 0:
                    copy_featT(L, NC - 1)
                    hidden(NC - 1)
                if L == 1:
                    normalise(NC - 1)
                    copy_featT(L, NC - 1)
                if L < 2:
                    new_features(L, NC - 1)
                    act.wait_ge(new_sb, (L + 1) * NC)
                    act.sem_inc(ab_ready, 1)

        @block.tensor
        def _(pe):
            mm, tr = nc.tensor.matmul, nc.tensor.transpose
            pe.wait_ge(dve_consts, 1)
            for k in range(NS):
                pe.wait_ge(before_ok, k + 1)
                for g in range(WG):
                    last = mm(ps[0:P, CNT + g:CNT + g + 1], before[:, k, P * g:P * (g + 1)], ones_b[:, :],
                              start=(k == 0 and g == 0), stop=(k == NS - 1), skip_group_check=True)
            last.then_inc(before_sum, 1)
            pe.wait_ge(weights_in, 16 * N_WEIGHTS)
            pe.wait_ge(consts, N_CONSTS)
            for k in range(KH):
                tr(ps[:, PREP + 128 * k:PREP + 128 * (k + 1)], w1[:, 128 * k:128 * (k + 1)], ident[:, :])
            for k in range(KH):
                tr(ps[:, PREP + 256 + 128 * k:PREP + 384 + 128 * k], w2[:, k, 0:D], ident[:, :])
            tr(ps[:, PREP + 512:PREP + 640], w3[:, 0:D], ident[:, :]).then_inc(prep_T, 1)
            pe.wait_ge(prep_sb, 1)
            for k in range(KH):
                mm(ps[:, VEC:VEC + 2], w1T[:, k, :], av1[:, k, :], start=(k == 0), stop=(k == KH - 1))
            for k in range(KH):
                mm(ps[:, VEC + 2 + 2 * k:VEC + 4 + 2 * k], w2T[:, k, :], av2[:, :], start=True, stop=True)
            mm(ps[:, VEC + 6:VEC + 8], w3T[:, :], av3[:, :], start=True, stop=True).then_inc(prep_v, 1)
            pe.wait_ge(g0_ready, 1)
            pe.wait_ge(prep_done, 1)
            for c in range(NC):
                if c:
                    pe.wait_ge(g0_sb, c)
                for t in range(CT):
                    last = tr(ps[0:D, 128 * t:128 * t + P], hA[:, c * CT + t, 0:D], ident[0:P, 0:P])
                last.then_inc(g0_T, 1)
                pe.wait_ge(g0_sb, c + 1)
                for t in range(CT):
                    n = AB0 + 2 * (c * CT + t)
                    last = mm(ps[0:P, n:n + 2], featT0[:, P * t:P * (t + 1)], w1v[:, :], start=True, stop=True)
                last.then_inc(ab0_ps, 1)
            pe.wait_ge(keys_ok, 2)
            for i, key in enumerate((k_lo, k_hi)):
                for k in range(KC):
                    for g in range(WG):
                        n = 128 * (WG * (KC * i + k) + g)
                        last = tr(ps[0:128, n:n + P], key[:, g, 128 * k:128 * (k + 1)], ident[0:P, 0:P])
            last.then_inc(keys_T, 1)
            mm(ps[0:P, COV:COV + 1], ones_f[:, :], covered[:, :], start=True, stop=True).then_inc(covered_sum, 1)

            def count(t, i):
                pe.wait_ge(hots_ok, t + 1)
                for j, (w0, w1_, at_) in enumerate(HALF):
                    pe.wait_ge(half_out[j], t)
                    for w in range(w0, w1_):
                        o = at_ + 128 * (w - w0)
                        for k in range(KC):
                            last = mm(ps[0:P, o:o + WC], hot_lo[i][:, :, KC * w + k], hot_col[i][:, :, KC * w + k],
                                      start=(k == 0), stop=(k == KC - 1))
                    last.then_inc(half_ok[j], 1)

            pe.wait_ge(keys_sb, 1)
            with pe.Fori(0, T - 1, 2) as t:
                count(t, 0)
                count(t + 1, 1)
            count(T - 1, 0)

            pe.wait_ge(flag_ok, 1)
            with pe.If(pe.value_load(general[0:1, 0:1], min_val=0, max_val=1)):
                HAND = EX // U
                pe.wait_ge(half_out[0], T)
                pe.wait_ge(half_out[1], T)
                with pe.Fori(0, P) as b:
                    pe.wait_ge(gen_out, b)
                    mm(ps[0:P, 0:512], zeros[:, 0:P], zeros[:, 0:512], start=True, stop=False)
                    mm(ps[0:P, 512:512 + P], zeros[:, 0:P], zeros[:, 0:P], start=True, stop=False)
                    with pe.Fori(0, HAND) as i:
                        pe.wait_ge(gen_hots, b * HAND + i + 1)
                        for u in range(U):
                            for w in range(WQ):
                                last = mm(ps[0:P, 128 * w:128 * w + WC], g_hot[:, u, 0, :], g_hot[:, u, 1 + w, :],
                                          start=False, stop=False, skip_group_check=True)
                        last.then_inc(gen_mm, 1)

            def top_transpose(L, c, first):
                n = L * NC + c
                pe.wait_ge(top_done, step_no(L, c, T))
                if not (L == 0 and first):
                    pe.wait_ge(top_max, n)
                for t in range(CT):
                    last = tr(ps[0:P, WORK + 128 * t:WORK + 128 * t + P], top_a[:, P * t:P * (t + 1)],
                              ident[0:P, 0:P])
                last.then_inc(top_T, 1)

            def rows(L, c, first):
                n = L * NC + c
                pe.wait_ge(uv_ready, n + 1)
                if not (L == 0 and first):
                    pe.wait_ge(e_ready, step_no(L, c, 0))
                for i, at_ in enumerate((ROWU, ROWV)):
                    for t in range(CT):
                        last = tr(ps[0:P, at_ + 128 * t:at_ + 128 * t + P],
                                  uv[:, i, t:t + 1].broadcast_to([P, P]), ident[0:P, 0:P])
                last.then_inc(rows_ready, 1)

            def products(L, A, feat, out_sem, last_of_group):
                for t in range(CT):
                    last = mm(ps[0:P, acc_at(t):acc_at(t) + HW], A[:, P * t:P * (t + 1)], feat,
                              start=False, stop=last_of_group, skip_group_check=last_of_group and t not in (2, CT - 1))
                last.then_inc(out_sem, 1)

            def rest_steps(L, c):
                with pe.If(pe.value_load(general[0:1, 0:1], min_val=0, max_val=1)):
                    with pe.Fori(0, T) as s:
                        pe.wait_ge(rest_p, step_no(L, c, s) + 1)
                        products(L, ringA[0], h_of[L][:, bass.ds(s, 1), :].rearrange("p o f -> p (o f)"),
                                 rest_pe, False)

            def feat_transposes(L, c, source, ready, n):
                pe.wait_ge(ready, n)
                pe.wait_ge(top_max, L * NC + c + 1)
                for t in range(CT):
                    last = tr(ps[0:D, WORK + 128 * t:WORK + 128 * t + P], source[:, t, :], ident[0:P, 0:P])
                last.then_inc(feat_T, 1)

            def hidden(c):
                pe.wait_ge(feat_sb, c + 1)
                for k in range(KH):
                    for t in range(CT):
                        o = WORK + 128 * (CT * k + t)
                        last = mm(ps[:, o:o + P], w1[:, 128 * k:128 * (k + 1)], featT[:, P * t:P * (t + 1)],
                                  start=True, stop=True)
                last.then_inc(h1_ps, 1)

            def new_features(L, c):
                if L == 0:
                    pe.wait_ge(h1_sb, c + 1)
                else:
                    pe.wait_ge(feat_sb, NC + c + 1)
                for t in range(CT):
                    o = ps[0:P, new_at(t):new_at(t) + AW]
                    if L == 0:
                        for k in range(KH):
                            last = mm(o, h1T[:, k, P * t:P * (t + 1)], w2[:, k, :], start=(k == 0),
                                      stop=(k == KH - 1))
                    else:
                        last = mm(o, featT[:, P * t:P * (t + 1)], w3[:, :], start=True, stop=True)
                last.then_inc(new_ps, 1)

            def chunk(L, c, first, last_chunk):
                if not (L == 0 and first):
                    pe.wait_ge(agg_ready, L * NC + c)
                for at_, n in ((0, 3 * HW), (512, 2 * HW)):
                    mm(ps[0:P, at_:at_ + n], zeros[:, 0:P], zeros[:, 0:n], start=True, stop=False)
                for s in range(T):
                    pe.wait_ge(p_ready, step_no(L, c, s) + 1)
                    products(L, ringA[s % RING], h_of[L][:, s, :], pe_done, s == T - 1)
                    if s == 4:
                        rest_steps(L, c)
                    if not first:
                        if L == 0 and s == 1:
                            feat_transposes(L, c - 1, agg, agg_ready, L * NC + c)
                        if L == 0 and s == 4:
                            hidden(c - 1)
                        if L == 0 and s == 7:
                            new_features(L, c - 1)
                        if L == 1 and s == 9:
                            feat_transposes(L, c - 1, gn, g_ready, c)
                        if L == 1 and s == 13:
                            new_features(L, c - 1)
                    if s == 17 and not last_chunk:
                        if L < 2 and not first:
                            pe.wait_ge(new_sb, L * NC + c)
                        top_transpose(L, c + 1, False)
                    if s == 22 and not last_chunk:
                        rows(L, c + 1, False)

            for L in range(LAYERS):
                if L:
                    pe.wait_ge(new_sb, L * NC)
                top_transpose(L, 0, True)
                rows(L, 0, True)
                chunk(L, 0, True, False)
                with pe.Fori(1, NC - 1) as c:
                    chunk(L, c, False, False)
                chunk(L, NC - 1, False, True)
                if L == 0:
                    feat_transposes(L, NC - 1, agg, agg_ready, (L + 1) * NC)
                    hidden(NC - 1)
                if L == 1:
                    feat_transposes(L, NC - 1, gn, g_ready, NC)
                if L < 2:
                    new_features(L, NC - 1)


def kernel(**inputs):
    import numpy as np
    import concourse.bacc as bacc
    from concourse import mybir as mb
    from concourse.bass_utils import run_bass_kernel_spmd

    arrays = {
        "x": inputs["x"],
        "edges": np.stack([inputs["src"], inputs["dst"]], axis=1),
        "W1": inputs["L0_gnn_W1"], "a_src1": inputs["L0_gnn_a_src1"], "a_dst1": inputs["L0_gnn_a_dst1"],
        "b1": inputs["L0_gnn_b1"],
        "W2": inputs["L0_gnn_W2"], "a_src2": inputs["L0_gnn_a_src2"], "a_dst2": inputs["L0_gnn_a_dst2"],
        "b2": inputs["L0_gnn_b2"],
        "W3": inputs["L1_gnn_W"], "a_src3": inputs["L1_gnn_att_src"], "a_dst3": inputs["L1_gnn_att_dst"],
        "b3": inputs["L1_gnn_bias"],
    }
    arrays = {n: np.ascontiguousarray(a) for n, a in arrays.items()}
    nc = bacc.Bacc("TRN2", target_bir_lowering=False, num_devices=1)
    aps = {n: nc.dram_tensor("in_" + n, a.shape, mb.dt.from_np(a.dtype), kind="ExternalInput").ap()
           for n, a in arrays.items()}
    out = nc.dram_tensor("out", inputs["x"].shape, mb.dt.float32, kind="ExternalOutput").ap()
    gat_stack_kernel(nc, out=out, **aps)
    r = run_bass_kernel_spmd(nc, [{"in_" + n: a for n, a in arrays.items()}], core_ids=[0])
    return r.results[0]["out"]
```

```python
from contextlib import ExitStack

import concourse.bass as bass
from concourse import mybir


def gat_stack_kernel(nc, x, edges, W1, a_src1, a_dst1, b1, W2, a_src2, a_dst2, b2,
                     W3, a_src3, a_dst3, b3, out):
    fp32, bf16 = mybir.dt.float32, mybir.dt.bfloat16
    i32, u8 = mybir.dt.int32, mybir.dt.uint8
    ALU, ACT, AX = mybir.AluOpType, mybir.ActivationFunctionType, mybir.AxisListType
    MAX_OVER_PARTITIONS = bass.bass_isa.ReduceOp.max

    N, D = x.shape
    E = edges.shape[0]
    H1 = W1.shape[1]
    KH = H1 // 128
    P = 125
    T = N // P
    WQ = 5
    NW = N // WQ
    WC = T * WQ
    WG = NW // P
    TW = P // WQ
    SLOTS = 256
    REAL = SLOTS - WQ
    KC = SLOTS // 128
    EP = E // P
    SAMPLE = 33
    NS = EP // SAMPLE
    CAP = 254
    CT = 5
    NC = T // CT
    CD = CT * P
    CW = CD // WQ
    RING = 5
    HW = D + 1
    AW = D + 2
    EX = EP + T
    U = 10
    EPS, SLOPE = 1e-5, 0.2
    SPAN_LIMIT = 110.0
    MAGIC = 12582912.0
    assert T * P == N and NW * WQ == N and WG * P == NW and EP * P == E and NS * SAMPLE == EP
    assert EX % U == 0 and WC == P

    x_v = x.rearrange("(t p) f -> p t f", p=P)
    out_v = out.rearrange("(t p) f -> p t f", p=P)
    rest_d = nc.dram_tensor("count_rest", (P, T, N), fp32).ap()

    ctx = ExitStack()
    with ctx:
        def sb(name, shape, dt=fp32):
            return ctx.enter_context(nc.sbuf_tensor(name, shape, dt))

        def sem(name):
            return ctx.enter_context(nc.semaphore(name))

        C = sb("C", [P, NW * WC], u8)
        C4 = C[:, :].rearrange("p (w t q) -> p w t q", t=T, q=WQ)
        xr = sb("xr", [P, T, D])
        hA = sb("hA", [P, T, HW])
        hB = sb("hB", [128, T * HW])
        hB3 = hB[0:P, :].rearrange("p (t f) -> p t f", f=HW)
        iota_t = hB[:, 0:P * TW * KC // 2].bitcast(bf16).rearrange("p (c n) -> p c n", c=P)
        scratch = sb("scratch", [128, 2 * P * TW * KC])
        edge_sb = sb("edge_sb", [P, EP, 2], i32)
        gathered = sb("gathered", [P, WG, SLOTS * 2], i32)
        gath4 = gathered[:, :, :].rearrange("p g (e c) -> p g e c", c=2)
        key_lo = sb("key_lo", [128, NW, KC], bf16)
        key_col = sb("key_col", [128, NW, KC], bf16)
        ident = sb("ident", [128, 128])
        w1 = sb("w1", [D, H1])
        w1T = sb("w1T", [128, KH, D])
        w1v = sb("w1v", [D, 2])
        w2 = sb("w2", [128, KH, AW])
        w2T = sb("w2T", [D, KH, 128])
        w3 = sb("w3", [D, AW])
        w3T = sb("w3T", [D, D])
        av1 = sb("av1", [128, KH, 2])
        av2 = sb("av2", [D, 2])
        av3 = sb("av3", [D, 2])
        b1c = sb("b1c", [128, KH])
        b2r = sb("b2r", [P, D])
        b3r = sb("b3r", [P, D])
        zeros = sb("zeros", [P, 512], bf16)
        ones_b = sb("ones_b", [P, 1], bf16)
        ones_f = sb("ones_f", [P, P])
        sampled = sb("sampled", [P, NS])
        win_base = sb("win_base", [P, WG])
        start_f = sb("start_f", [P, WG])
        start_i = sb("start_i", [P, WG], i32)
        covered = sb("covered", [P, 1])
        covers = sb("covers", [P, 1])
        general = sb("general", [1, 1], i32)
        careful = sb("careful", [1, 1], i32)
        bn6 = sb("bn6", [P, T, 6])
        mv = sb("mv", [P, T, 2])
        bn6c = sb("bn6c", [P, CT, 6])
        mvc = sb("mvc", [P, CT, 2])
        rstd = sb("rstd", [P, T])
        nbias = sb("nbias", [P, T])
        neghalf = sb("neghalf", [P, T])
        ab = [sb(f"ab{L}", [P, T, 2]) for L in range(3)]
        ext = sb("ext", [P, 2])
        extg = sb("extg", [P, 2])
        span = sb("span", [P, 3])
        a_unit = sb("a_unit", [P, T])
        a_neg = sb("a_neg", [P, T])
        a_leak = sb("a_leak", [P, T])
        b_low = sb("b_low", [P, T])
        a_top = sb("a_top", [P, 1])
        is_fast = sb("is_fast", [P, 2])
        b_cut = sb("b_cut", [P, T])
        b_rest = sb("b_rest", [P, T])
        shift = sb("shift", [P, 1])
        floor = sb("floor", [P, T])
        to_relu = sb("to_relu", [P, T])
        to_exp = sb("to_exp", [P, T])
        row_fast = sb("row_fast", [P, T])
        back_fast = sb("back_fast", [P, T])
        mu = sb("mu", [P, CT])
        e_top = sb("e_top", [P, CT])
        m_top = sb("m_top", [P, CT])
        uv = sb("uv", [P, 2, CT])
        back = sb("back", [P, CT])
        kappa = sb("kappa", [P, T])
        zk = sb("zk", [P, 3, CT])
        rz = sb("rz", [P, CT])
        featT0 = sb("featT0", [D, CT * P])

        sc_b = scratch[:, :].bitcast(bf16)
        win_dst = hA[:, :, :].rearrange("p t f -> p (t f)")[:, 0:NW]
        before = sc_b[0:P, 0:NS * NW].rearrange("p (k w) -> p k w", k=NS)
        NSL = WG * SLOTS

        def slot_plane(i):
            return scratch[0:P, i * NSL:(i + 1) * NSL].rearrange("p (g e) -> p g e", g=WG)

        k_hi, k_lo, k_dl, k_ok, k_in = (slot_plane(i) for i in range(5))
        OH = P * TW * KC
        hot_lo = [sc_b[:, 2 * i * OH:(2 * i + 1) * OH].rearrange("p (c n) -> p c n", c=P) for i in range(2)]
        hot_col = [sc_b[:, (2 * i + 1) * OH:(2 * i + 2) * OH].rearrange("p (c n) -> p c n", c=P) for i in range(2)]
        g_lo, g_col, g_hi, g_dst, g_win, g_shift = (scratch[0:P, i * EX:(i + 1) * EX] for i in range(6))
        g_at = 6 * EX
        g_iota = scratch[0:P, g_at:g_at + WQ * WC]
        g_plane = scratch[0:P, g_at + 640:g_at + 640 + WQ * WC]
        g_hot = scratch[0:P, g_at + 1280:g_at + 1280 + U * 3 * P].bitcast(bf16).rearrange(
            "p (u k c) -> p u k c", u=U, k=6)
        ringA = [scratch[0:P, i * CD:(i + 1) * CD] for i in range(RING)]
        ringB = [scratch[0:P, (RING + i) * CD:(RING + i + 1) * CD] for i in range(RING)]
        at = 2 * RING * CD
        top_a = scratch[0:P, at:at + CD]
        rest_sb = scratch[0:P, at + CD:at + 2 * CD]
        at += 2 * CD
        raw = scratch[0:P, at:at + CT * HW].rearrange("p (t f) -> p t f", f=HW)
        at += CT * HW
        agg = scratch[0:P, at:at + CT * D].rearrange("p (t f) -> p t f", f=D)
        at += CT * D
        gn = scratch[0:P, at:at + CT * D].rearrange("p (t f) -> p t f", f=D)
        at += CT * D
        featT = scratch[0:D, at:at + CD]
        at += CD
        h1T = scratch[:, at:at + KH * CD].rearrange("p (k n) -> p k n", k=KH)
        at += KH * CD
        c_bf = scratch[0:P, at:at + CD // 2 + 1].bitcast(bf16)[:, 0:CD]
        assert at + CD <= 2 * OH and g_at + 1280 + U * 3 * P <= 2 * OH and NS * NW <= 4 * OH

        ps = ctx.enter_context(nc.psum_tensor("ps", [128, 8 * 512], fp32))

        def tiles(at, n=CT, width=P, rows=P):
            return ps[0:rows, at:at + 128 * n].rearrange("p (t c) -> p t c", c=128)[:, :, 0:width]

        def acc_at(t):
            return 512 * (t // 3) + HW * (t % 3)

        ROWU, ROWV, WORK = 1024, 1024 + 128 * CT, 2560

        def new_at(t):
            return WORK + 512 * (t // 3) + AW * (t % 3)

        acc3 = [ps[0:P, 0:3 * HW].rearrange("p (t f) -> p t f", f=HW),
                ps[0:P, 512:512 + 2 * HW].rearrange("p (t f) -> p t f", f=HW)]
        new3 = [ps[0:P, WORK:WORK + 3 * AW].rearrange("p (t f) -> p t f", f=AW),
                ps[0:P, WORK + 512:WORK + 512 + 2 * AW].rearrange("p (t f) -> p t f", f=AW)]
        PREP, VEC, AB0, CNT, COV = 2560, 2048, 1792, 3584, 3648
        G0T = [3584 + 128 * t for t in range(4)] + [1664]
        HALF = [(0, (TW + 1) // 2, 0), ((TW + 1) // 2, TW, 2048)]

        edges_in = sem("edges_in")
        x_in = sem("x_in")
        weights_in = sem("weights_in")
        consts = sem("consts")
        iota_ready = sem("iota_ready")
        dve_consts = sem("dve_consts")
        samples_ok = sem("samples_ok")
        before_ok = sem("before_ok")
        before_sum = sem("before_sum")
        start_lin = sem("start_lin")
        starts_ok = sem("starts_ok")
        gather_in = sem("gather_in")
        keys_lin = sem("keys_lin")
        keys_ok = sem("keys_ok")
        covered_sum = sem("covered_sum")
        flag_ok = sem("flag_ok")
        keys_T = sem("keys_T")
        keys_sb = sem("keys_sb")
        prep_T = sem("prep_T")
        prep_sb = sem("prep_sb")
        prep_v = sem("prep_v")
        prep_done = sem("prep_done")
        hots_ok = sem("hots_ok")
        half_ok = [sem("half0_ok"), sem("half1_ok")]
        half_out = [sem("half0_out"), sem("half1_out")]
        ones_col = sem("ones_col")
        gen_lin = sem("gen_lin")
        gen_hots = sem("gen_hots")
        gen_zero = sem("gen_zero")
        gen_mm = sem("gen_mm")
        gen_sum = sem("gen_sum")
        gen_out = sem("gen_out")
        gen_plane = sem("gen_plane")
        gen_stored = sem("gen_stored")
        counts_done = sem("counts_done")
        ln_lin = sem("ln_lin")
        ln_stats = sem("ln_stats")
        ln_pool = sem("ln_pool")
        ln_ready = sem("ln_ready")
        g0_ready = sem("g0_ready")
        g0_T = sem("g0_T")
        g0_sb = sem("g0_sb")
        ab0_ps = sem("ab0_ps")
        ab_ready = sem("ab_ready")
        ext_lin = sem("ext_lin")
        prep_lin = sem("prep_lin")
        shift_ready = sem("shift_ready")
        floor_ready = sem("floor_ready")
        mode_ready = sem("mode_ready")
        fast_ready = sem("fast_ready")
        back_ready = sem("back_ready")
        kappa_ready = sem("kappa_ready")
        raw_ready = sem("raw_ready")
        raw_used = sem("raw_used")
        z_lin = sem("z_lin")
        ext_ready = sem("ext_ready")
        extg_ready = sem("extg_ready")
        scal_lin = sem("scal_lin")
        scal_ready = sem("scal_ready")
        e_ready = sem("e_ready")
        e_pool = [sem(f"e_pool{L}") for L in range(3)]
        relu_done = [sem(f"relu_done{L}") for L in range(3)]
        counts_bf = sem("counts_bf")
        x_ready = sem("x_ready")
        q_ready = sem("q_ready")
        b2_added = sem("b2_added")
        mx_done = [sem(f"mx_done{L}") for L in range(3)]
        p_ready = sem("p_ready")
        pe_done = sem("pe_done")
        top_done = sem("top_done")
        top_T = sem("top_T")
        top_max = sem("top_max")
        m_lin = sem("m_lin")
        uv_ready = sem("uv_ready")
        rows_ready = sem("rows_ready")
        rz_ready = sem("rz_ready")
        feat_T = sem("feat_T")
        feat_sb = sem("feat_sb")
        h1_ps = sem("h1_ps")
        h1_sb = sem("h1_sb")
        new_ps = sem("new_ps")
        new_sb = sem("new_sb")
        res_lin = sem("res_lin")
        g_ready = sem("g_ready")
        y_ready = sem("y_ready")
        out_done = sem("out_done")
        rest_in = sem("rest_in")
        rest_e = sem("rest_e")
        rest_mx = sem("rest_mx")
        rest_p = sem("rest_p")
        rest_pe = sem("rest_pe")

        N_WEIGHTS, N_CONSTS = 15, 6
        VEC_TOPS = 3
        TOPS_FROM = 3
        CHAIN_AT = (2, 3, 4, 5)
        ROW_AT, ROWS_PE = 16, 20
        KAPPA_AT = 8
        Z_AT = (8, 9, 10)
        RESIDUAL_AT, STATS = 10, (12, 13)
        POST_POOL = [((9, 0),), ((14, 3),), ((12, 0), (15, 1), (18, 2))]
        POST_PE = [(10, 13, 16), (15, None, 17), (None, None, None)]
        POST_ACT = [(15, 18, 21), (17, 19, 21), (None, None, None)]
        LAYERS = 3
        h_of = [hA[:, :, :], hB3, hA[:, :, :]]
        new_of = [hB3, hA[:, :, :], None]

        def step_no(L, c, s):
            return (L * NC + c) * T + s

        POOL_S = tuple(range(2, T - 1, 3))

        def pool_before(s):
            return sum(1 for i in POOL_S if i < s)

        def pool_no(L, c, s):
            return (L * NC + c) * len(POOL_S) + pool_before(s)

        def dve_no(L, c, s):
            return (L * NC + c) * (T - len(POOL_S)) + s - pool_before(s)

        block = ctx.enter_context(nc.Block())

        @block.sync
        def _(sp):
            sp.dma_start(edge_sb[:, :, :], edges.rearrange("(p k) c -> p k c", p=P)).then_inc(edges_in, 16)
            sp.dma_start(xr[:, :, :], x_v).then_inc(x_in, 16)
            sp.dma_start(w1[:, :], W1).then_inc(weights_in, 16)
            sp.dma_start(w2[:, :, 0:D], W2.rearrange("(k p) f -> p k f", p=128)).then_inc(weights_in, 16)
            sp.dma_start(w3[:, 0:D], W3).then_inc(weights_in, 16)
            for k in range(KH):
                sp.dma_start(b1c[:, k:k + 1], b1[128 * k:128 * (k + 1)].unsqueeze(1)).then_inc(weights_in, 16)
            for i, a in enumerate((a_src1, a_dst1)):
                for k in range(KH):
                    sp.dma_start(av1[:, k, i:i + 1], a[128 * k:128 * (k + 1)].unsqueeze(1)).then_inc(weights_in, 16)
            for v, pair in ((av2, (a_src2, a_dst2)), (av3, (a_src3, a_dst3))):
                for i, a in enumerate(pair):
                    sp.dma_start(v[:, i:i + 1], a.unsqueeze(1)).then_inc(weights_in, 16)
            sp.dma_start(b2r[:, :], b2.unsqueeze(0).broadcast_to([P, D])).then_inc(weights_in, 16)
            sp.dma_start(b3r[:, :], b3.unsqueeze(0).broadcast_to([P, D])).then_inc(weights_in, 16)

            sp.wait_ge(flag_ok, 1)
            with sp.If(sp.value_load(general[0:1, 0:1], min_val=0, max_val=1)):
                with sp.Fori(0, P) as b:
                    first = sp.snap(b * WQ * WQ)
                    sp.wait_ge(gen_plane, b + 1)
                    sp.dma_start(rest_d[:, :, bass.ds(first, WQ * WQ)],
                                 g_plane.rearrange("p (t d) -> p t d", t=T)).then_inc(gen_stored, 16)

            def rest_loads(L, c):
                with sp.If(sp.value_load(general[0:1, 0:1], min_val=0, max_val=1)):
                    sp.wait_ge(gen_stored, 16 * P)
                    with sp.Fori(0, T) as s:
                        tile, first = sp.snap(s + 0), sp.snap(c * CD)
                        sp.wait_ge(rest_pe, step_no(L, c, s))
                        sp.wait_ge(counts_done, 1)
                        sp.dma_start(rest_sb, rest_d[:, bass.ds(tile, 1), bass.ds(first, CD)].rearrange(
                            "p t d -> p (t d)")).then_inc(rest_in, 16)

            def store(c):
                sp.wait_ge(y_ready, c + 1)
                sp.dma_start(out_v[:, bass.ds(c * CT, CT), :], xr[:, bass.ds(c * CT, CT), :]).then_inc(out_done, 16)

            for L in range(LAYERS - 1):
                with sp.Fori(0, NC) as c:
                    rest_loads(L, c)
            for c in range(NC):
                if c:
                    store(c - 1)
                rest_loads(LAYERS - 1, c)
            store(NC - 1)
            sp.wait_ge(out_done, 16 * NC)

        @block.gpsimd
        def _(pool):
            g = nc.gpsimd
            g.iota(win_dst, [[WQ, NW]], 0, channel_multiplier=0,
                   allow_small_or_imprecise_dtypes=True).then_inc(consts, 1)
            g.iota(win_base[:, :], [[WQ * P, WG]], 0, channel_multiplier=WQ,
                   allow_small_or_imprecise_dtypes=True).then_inc(consts, 1)
            g.iota(gath4[:, :, REAL:SLOTS, :], [[WQ * P, WG], [1, WQ], [0, 2]], 0,
                   channel_multiplier=WQ).then_inc(consts, 1)
            g.memset(ident[:, :], 1.0).then_inc(consts, 1)
            pool.wait_ge(consts, 4)
            g.affine_select(out=ident[:, :], in_=ident[:, :], compare_op=ALU.is_equal, fill=0.0, base=0,
                            pattern=[[-1, 128]], channel_multiplier=1).then_inc(consts, 1)
            g.memset(neghalf[:, :], -0.5).then_inc(consts, 1)
            g.iota(iota_t, [[1, P], [0, TW * KC]], 0, channel_multiplier=0,
                   allow_small_or_imprecise_dtypes=True).then_inc(iota_ready, 1)
            pool.wait_ge(consts, N_CONSTS)
            pool.wait_ge(starts_ok, 1)
            for i in range(WG):
                g.indirect_dma_start(gathered[:, i, 0:2 * REAL], None, edges,
                                     bass.IndirectOffsetOnAxis(ap=start_i[:, i:i + 1], axis=0)
                                     ).then_inc(gather_in, 16)

            def norm_scalars(var, mean, r, nb, half, n):
                g.tensor_scalar(r, var, EPS, None, ALU.add).then_inc(ln_pool, 1)
                pool.wait_ge(ln_pool, n + 1)
                g.tensor_tensor(r, r, half, ALU.pow).then_inc(ln_pool, 1)
                g.tensor_scalar(nb, mean, -1.0, None, ALU.mult).then_inc(ln_pool, 1)
                pool.wait_ge(ln_pool, n + 3)
                g.tensor_tensor(nb, nb, r, ALU.mult).then_inc(ln_ready, 1)

            pool.wait_ge(ln_stats, 1)
            norm_scalars(mv[:, :, 1], mv[:, :, 0], rstd[:, :], nbias[:, :], neghalf[:, :], 0)

            def extremes(L):
                pool.wait_ge(ext_ready, L + 1)
                g.partition_all_reduce(extg[:, :], ext[:, :], P, MAX_OVER_PARTITIONS).then_inc(extg_ready, 1)

            def blocks(L, c, s0, s1):
                for s in POOL_S:
                    if s0 <= s < s1:
                        A = ringA[s % RING]
                        pool.wait_ge(counts_bf, pool_no(L, c, s) + 1)
                        pool.wait_ge(x_ready, pool_no(L, c, s) + 1)
                        g.tensor_tensor(A, A, c_bf, ALU.mult).then_inc(q_ready, 1)
                        pool.wait_ge(q_ready, pool_no(L, c, s) + 1)
                        i = POOL_S.index(s) + 1
                        if i < len(POOL_S):
                            widen(c, POOL_S[i])
                        elif L * NC + c + 1 < LAYERS * NC:
                            widen((c + 1) % NC, POOL_S[0])

            def widen(c, s):
                g.tensor_copy(c_bf.rearrange("p (w q) -> p w q", q=WQ),
                              C4[:, c * CW:(c + 1) * CW, s, :]).then_inc(counts_bf, 1)

            def scaled_sums(c):
                pool.wait_ge(rz_ready, c + 1)
                pool.wait_ge(feat_T, c)
                g.tensor_tensor(agg, raw[:, :, 0:D], rz[:, :].unsqueeze(2).broadcast_to([P, CT, D]),
                                ALU.mult).then_inc(raw_used, 1)

            def result(c, part):
                n = (LAYERS - 1) * NC + c
                xc = xr[:, c * CT:(c + 1) * CT, :]
                if part == 0:
                    pool.wait_ge(rz_ready, n + 1)
                    g.tensor_tensor(agg, raw[:, :, 0:D], rz[:, :].unsqueeze(2).broadcast_to([P, CT, D]),
                                    ALU.mult).then_inc(raw_used, 1)
                elif part == 1:
                    pool.wait_ge(raw_used, n + 1)
                    g.tensor_tensor(xc, xc, agg, ALU.add).then_inc(res_lin, 1)
                else:
                    pool.wait_ge(res_lin, c + 1)
                    g.tensor_tensor(xc, xc, b3r[:, :].unsqueeze(1).broadcast_to([P, CT, D]),
                                    ALU.add).then_inc(y_ready, 1)

            def post(L, c, part):
                if L == 0:
                    scaled_sums(c)
                elif L == 2:
                    result(c, part)
                else:
                    pool.wait_ge(ln_stats, c + 2)
                    pool.wait_ge(g_ready, c)
                    norm_scalars(mvc[:, :, 1], mvc[:, :, 0], rstd[:, 0:CT], nbias[:, 0:CT],
                                 neghalf[:, 0:CT], c * 3 + 3)

            pool.wait_ge(weights_in, 16 * N_WEIGHTS)
            pool.wait_ge(g0_ready, 1)
            g.tensor_tensor(xr[:, :, :], xr[:, :, :], b2r[:, :].unsqueeze(1).broadcast_to([P, T, D]),
                            ALU.add).then_inc(b2_added, 1)
            pool.wait_ge(hots_ok, T)
            g.memset(hB3[:, :, D:HW], 1.0).then_inc(ones_col, 1)
            pool.wait_ge(b2_added, 1)
            pool.wait_ge(counts_done, 1)
            widen(0, POOL_S[0])
            for L in range(LAYERS):
                extremes(L)
                for c in range(NC):
                    s = 0
                    for at_, part in POST_POOL[L]:
                        blocks(L, c, s, at_)
                        if c:
                            post(L, c - 1, part)
                        s = at_
                    blocks(L, c, s, T)
                for _at, part in POST_POOL[L]:
                    post(L, NC - 1, part)

        @block.vector
        def _(dve):
            v = nc.vector
            v.memset(ones_b[:, :], 1.0)
            v.memset(ones_f[:, :], 1.0)
            v.memset(zeros[:, :], 0.0).then_inc(dve_consts, 1)
            dve.wait_ge(edges_in, 16)
            v.tensor_copy(sampled[:, :], edge_sb[:, :, :].rearrange("p (k r) c -> p k r c", r=SAMPLE)[:, :, 0, 1]
                          ).then_inc(samples_ok, 1)
            dve.wait_ge(samples_ok, 1)
            dve.wait_ge(consts, N_CONSTS)
            for k in range(NS):
                v.tensor_scalar(before[:, k, :], win_dst, sampled[:, k:k + 1], None,
                                ALU.is_gt).then_inc(before_ok, 1)
            dve.wait_ge(before_sum, 1)
            v.tensor_scalar(start_f[:, :], ps[0:P, CNT:CNT + WG], float(SAMPLE), float(1 - SAMPLE),
                            ALU.mult, ALU.add).then_inc(start_lin, 1)
            dve.wait_ge(start_lin, 1)
            v.tensor_scalar(start_i[:, :], start_f[:, :], 0.0, float(E - REAL), ALU.max,
                            ALU.min).then_inc(starts_ok, 1)
            dve.wait_ge(x_in, 16)
            for t in range(T):
                last = v.bn_stats(bn6[:, t, :], xr[:, t, :])
            last.then_inc(ln_lin, 1)
            dve.wait_ge(ln_lin, 1)
            for t in range(T):
                last = v.bn_aggr(mv[:, t, :], bn6[:, t, :])
            last.then_inc(ln_stats, 1)
            v.memset(hA[:, :, D:HW], 1.0).then_inc(dve_consts, 1)
            dve.wait_ge(gather_in, 16 * WG)
            src, dst = gath4[:, :, :, 0], gath4[:, :, :, 1]
            v.tensor_scalar(k_hi, src, 1.0 / P, -0.5 + 0.5 / P, ALU.mult, ALU.add).then_inc(keys_lin, 1)
            v.tensor_tensor(k_dl, dst, win_base[:, :].unsqueeze(2).broadcast_to([P, WG, SLOTS]),
                            ALU.subtract).then_inc(keys_lin, 1)
            dve.wait_ge(keys_lin, 1)
            v.tensor_scalar(k_hi, k_hi, MAGIC, MAGIC, ALU.add, ALU.subtract).then_inc(keys_lin, 1)
            dve.wait_ge(keys_lin, 2)
            v.tensor_scalar(k_in, k_dl, 0.0, None, ALU.is_ge).then_inc(keys_lin, 1)
            dve.wait_ge(keys_lin, 3)
            v.scalar_tensor_tensor(k_lo, k_hi, -float(P), src, ALU.mult, ALU.add).then_inc(keys_lin, 1)
            dve.wait_ge(keys_lin, 4)
            v.scalar_tensor_tensor(k_ok, k_dl, float(WQ - 1), k_in, ALU.is_le, ALU.mult).then_inc(keys_lin, 1)
            v.scalar_tensor_tensor(k_hi, k_hi, float(WQ), k_dl, ALU.mult, ALU.add).then_inc(keys_lin, 1)
            dve.wait_ge(keys_lin, 7)
            v.scalar_tensor_tensor(k_hi, k_hi, 1.0, k_ok, ALU.add, ALU.mult).then_inc(keys_ok, 1)
            v.tensor_reduce(covered[:, :], k_ok, AX.XY, ALU.add).then_inc(keys_ok, 1)
            dve.wait_ge(covered_sum, 1)
            v.tensor_scalar(covers[:, :], ps[0:P, COV:COV + 1], float(E + N), None, ALU.is_equal)
            v.tensor_scalar(general[0:1, 0:1], ps[0:1, COV:COV + 1], float(E + N), None,
                            ALU.not_equal).then_inc(flag_ok, 1)
            dve.wait_ge(iota_ready, 1)
            dve.wait_ge(keys_sb, 1)

            def one_hots(t, i, behind):
                if behind:
                    dve.wait_ge(half_ok[1], t - 1)
                for hot, key in ((hot_lo[i], key_lo), (hot_col[i], key_col)):
                    keys = key[:, bass.ds(t * TW, TW), :].rearrange("p w k -> p (w k)")
                    last = v.tensor_tensor(hot, keys.unsqueeze(1).broadcast_to([128, P, TW * KC]), iota_t,
                                           ALU.is_equal)
                last.then_inc(hots_ok, 1)

            one_hots(0, 0, False)
            one_hots(1, 1, False)
            with dve.Fori(2, T - 1, 2) as t:
                one_hots(t, 0, True)
                one_hots(t + 1, 1, True)
            one_hots(T - 1, 0, True)
            dve.wait_ge(half_out[0], T)
            dve.wait_ge(half_out[1], T)

            dve.wait_ge(flag_ok, 1)
            with dve.If(dve.value_load(general[0:1, 0:1], min_val=0, max_val=1)):
                n = [0]

                def then(ins):
                    n[0] += 1
                    ins.then_inc(gen_lin, 1)
                    dve.wait_ge(gen_lin, n[0])

                then(v.memset(g_win, 0.0))
                then(v.tensor_copy(g_lo[:, 0:EP], edge_sb[:, :, 0]))
                then(v.tensor_copy(g_dst[:, 0:EP], edge_sb[:, :, 1]))
                for t in range(T):
                    then(v.tensor_scalar(g_lo[:, EP + t:EP + t + 1], win_base[:, 0:1], 1.0 / WQ, float(P * t),
                                         ALU.mult, ALU.add))
                then(v.tensor_scalar(g_lo[:, EP:EX], g_lo[:, EP:EX], MAGIC, MAGIC, ALU.add, ALU.subtract))
                then(v.tensor_copy(g_dst[:, EP:EX], g_lo[:, EP:EX]))
                then(v.tensor_scalar(g_hi, g_lo, 1.0 / P, -0.5 + 0.5 / P, ALU.mult, ALU.add))
                then(v.tensor_scalar(g_hi, g_hi, MAGIC, MAGIC, ALU.add, ALU.subtract))
                then(v.scalar_tensor_tensor(g_lo, g_hi, -float(P), g_lo, ALU.mult, ALU.add))
                then(v.tensor_scalar(g_win, g_dst, 1.0 / WQ, -0.5 + 0.5 / WQ, ALU.mult, ALU.add))
                then(v.tensor_scalar(g_win, g_win, MAGIC, MAGIC, ALU.add, ALU.subtract))
                then(v.scalar_tensor_tensor(g_col, g_hi, float(WQ), g_dst, ALU.mult, ALU.add))
                then(v.scalar_tensor_tensor(g_col, g_win, float(WC - WQ), g_col, ALU.mult, ALU.add))
                for w in range(WQ):
                    then(v.tensor_copy(g_iota[:, WC * w:WC * (w + 1)], win_dst[:, 0:WC]))
                    then(v.tensor_scalar(g_iota[:, WC * w:WC * (w + 1)], g_iota[:, WC * w:WC * (w + 1)],
                                         1.0 / WQ, float(WC * w), ALU.mult, ALU.add))
                then(v.tensor_scalar(g_iota, g_iota, MAGIC, MAGIC, ALU.add, ALU.subtract))
                then(v.tensor_copy(g_shift, g_col))
                HAND = EX // U
                with dve.Fori(0, P) as b:
                    with dve.Fori(0, HAND) as i:
                        dve.wait_ge(gen_mm, b * HAND + i)
                        for u in range(U):
                            e = bass.ds(i * U + u, 1)
                            v.tensor_scalar(g_hot[:, u, 0, :], g_iota[:, 0:P], g_lo[:, e], None, ALU.is_equal)
                            last = v.tensor_scalar(g_hot[:, u, 1:6, :].rearrange("p k c -> p (k c)"), g_iota,
                                                   g_shift[:, e], None, ALU.is_equal)
                        last.then_inc(gen_hots, 1)
                    dve.wait_ge(gen_sum, b + 1)
                    v.tensor_scalar(C[:, bass.ds(b * WQ * WC, WQ * WC)].rearrange("p (w c) -> p w c", w=WQ),
                                    tiles(0, WQ), float(CAP), None, ALU.min)
                    dve.wait_ge(gen_stored, b * 16)
                    for w in range(WQ):
                        last = v.tensor_scalar(
                            g_plane.rearrange("p (t w q) -> p t w q", t=T, w=WQ)[:, :, w, :],
                            ps[0:P, 128 * w:128 * w + WC].rearrange("p (t q) -> p t q", q=WQ),
                            float(CAP), float(CAP), ALU.max, ALU.subtract)
                    last.then_inc(gen_plane, 1)
                    v.tensor_scalar(g_shift, g_shift, -float(WQ * WC), None, ALU.add).then_inc(gen_out, 1)
                    dve.wait_ge(gen_out, b + 1)
                dve.wait_ge(gen_stored, 16 * P)
            v.memset(rz[:, :], 0.0).then_inc(counts_done, 1)

            def scalars(L):
                a, b = ab[L][:, :, 0], ab[L][:, :, 1]
                dve.wait_ge(ab_ready, L + 1)
                v.tensor_scalar(a_neg[:, :], a, -1.0, None, ALU.mult).then_inc(ext_lin, 1)
                v.tensor_reduce(ext[:, 0:1], a, AX.X, ALU.max)
                dve.wait_ge(ext_lin, L + 1)
                v.tensor_reduce(ext[:, 1:2], a_neg[:, :], AX.X, ALU.max).then_inc(ext_ready, 1)
                v.tensor_scalar(a_leak[:, :], a, SLOPE, None, ALU.mult)
                dve.wait_ge(extg_ready, L + 1)
                v.tensor_tensor(span[:, 0:1], extg[:, 0:1], extg[:, 1:2], ALU.add).then_inc(scal_lin, 1)
                v.tensor_scalar(b_low[:, :], b, extg[:, 1:2], None, ALU.subtract)
                dve.wait_ge(scal_lin, 3 * L + 1)
                v.tensor_scalar(span[:, 1:2], span[:, 0:1], 1e-30, None, ALU.max).then_inc(scal_lin, 1)
                dve.wait_ge(scal_lin, 3 * L + 2)
                v.reciprocal(span[:, 2:3], span[:, 1:2]).then_inc(scal_lin, 1)
                dve.wait_ge(scal_lin, 3 * L + 3)
                v.tensor_scalar(a_unit[:, :], a, extg[:, 1:2], span[:, 2:3], ALU.add,
                                ALU.mult).then_inc(scal_ready, 1)
                dve.wait_ge(scal_ready, L + 1)

            def layer_vectors(L, part):
                b = ab[L][:, :, 1]
                if part == 0:
                    v.tensor_scalar(a_top[:, :], extg[:, 0:1], -SLOPE, None, ALU.mult)
                    v.tensor_scalar(is_fast[:, 0:1], span[:, 0:1], SPAN_LIMIT, covers[:, :], ALU.is_le, ALU.mult)
                    v.tensor_scalar(b_cut[:, :], b, extg[:, 1:2], 1.0 - SLOPE, ALU.min,
                                    ALU.mult).then_inc(prep_lin, 1)
                elif part == 1:
                    dve.wait_ge(prep_lin, 2 * L + 1)
                    v.scalar_tensor_tensor(shift[:, :], span[:, 0:1], -(1.0 - SLOPE) / 2, a_top[:, :], ALU.mult,
                                           ALU.add).then_inc(shift_ready, 1)
                    v.tensor_scalar(is_fast[:, 1:2], is_fast[:, 0:1], -1.0, None, ALU.mult)
                    v.tensor_scalar(careful[:, :], is_fast[0:1, 0:1], 0.0, None, ALU.is_equal).then_inc(mode_ready, 1)
                    v.tensor_tensor(b_rest[:, :], b, b_cut[:, :], ALU.subtract).then_inc(prep_lin, 1)
                else:
                    dve.wait_ge(prep_lin, 2 * L + 2)
                    a = ab[L][:, :, 0]
                    v.tensor_scalar(to_relu[:, :], a, 1.0 - SLOPE, shift[:, :], ALU.mult, ALU.subtract)
                    v.tensor_scalar(to_exp[:, :], a, SLOPE, shift[:, :], ALU.mult, ALU.add)
                    v.tensor_scalar(row_fast[:, :], b_cut[:, :], shift[:, :], is_fast[:, 0:1], ALU.add, ALU.mult)
                    v.tensor_scalar(back_fast[:, :], b_rest[:, :], shift[:, :], is_fast[:, 0:1], ALU.subtract,
                                    ALU.mult).then_inc(fast_ready, 1)

            def top_step(L, c, s):
                counts = C4[:, bass.ds(c * CW, CW), s, :]
                top = top_a.rearrange("p (w q) -> p w q", q=WQ)
                if s == 0:
                    if not (L == 0 and isinstance(c, int) and c == 0):
                        dve.wait_ge(top_T, L * NC + c)
                    v.tensor_scalar(top, counts, a_unit[:, 0:1], None, ALU.min).then_inc(top_done, 1)
                else:
                    dve.wait_ge(top_done, step_no(L, c, s))
                    v.scalar_tensor_tensor(top, counts, a_unit[:, s:s + 1], top, ALU.min,
                                           ALU.max).then_inc(top_done, 1)

            def maxima(L, c, first, part):
                n = L * NC + c
                tc = bass.ds(c * CT, CT)
                if part == 0:
                    dve.wait_ge(top_T, n + 1)
                    v.tensor_reduce(mu[:, :], tiles(WORK), AX.X, ALU.max).then_inc(top_max, 1)
                elif part == 1:
                    dve.wait_ge(top_max, n + 1)
                    v.scalar_tensor_tensor(e_top[:, :], mu[:, :], span[:, 1:2], b_low[:, tc], ALU.mult,
                                           ALU.add).then_inc(m_lin, 1)
                elif part == 2:
                    dve.wait_ge(m_lin, 2 * n + 1)
                    v.scalar_tensor_tensor(m_top[:, :], e_top[:, :], SLOPE, e_top[:, :], ALU.mult,
                                           ALU.max).then_inc(m_lin, 1)
                else:
                    dve.wait_ge(m_lin, 2 * n + 2)
                    dve.wait_ge(fast_ready, L + 1)
                    if not (L == 0 and first):
                        dve.wait_ge(kappa_ready, n)
                    v.scalar_tensor_tensor(back[:, :], m_top[:, :], is_fast[:, 1:2], back_fast[:, tc], ALU.mult,
                                           ALU.add).then_inc(back_ready, 1)

            def row_columns(L, c, first, two_exps):
                n = L * NC + c
                tc = bass.ds(c * CT, CT)
                if not (L == 0 and first):
                    dve.wait_ge(rows_ready, n)
                if two_exps:
                    v.tensor_tensor(uv[:, 0, :], ab[L][:, tc, 1], m_top[:, :], ALU.subtract)
                    v.scalar_tensor_tensor(uv[:, 1, :], ab[L][:, tc, 1], SLOPE, m_top[:, :], ALU.mult,
                                           ALU.subtract).then_inc(uv_ready, 1)
                else:
                    v.tensor_copy(uv[:, 0, :], row_fast[:, tc]).then_inc(uv_ready, 1)

            def sums_inverse(L, c, part):
                n = L * NC + c
                z, r = zk[:, 1, :] if L == LAYERS - 1 else zk[:, 0, :], zk[:, 2, :]
                scale = kappa[:, bass.ds(c * CT, CT)]
                if part == 0:
                    dve.wait_ge(raw_ready, n + 1)
                    dve.wait_ge(kappa_ready, n + 1)
                    v.tensor_tensor(zk[:, 0, :], raw[:, :, D], scale, ALU.mult).then_inc(z_lin, 1)
                elif part == 1:
                    dve.wait_ge(z_lin, 3 * n + 1)
                    if L == LAYERS - 1:
                        v.tensor_scalar(z, zk[:, 0, :], 1e-16, None, ALU.add).then_inc(z_lin, 1)
                        dve.wait_ge(z_lin, 3 * n + 2)
                        v.reciprocal(r, z).then_inc(z_lin, 1)
                    else:
                        v.reciprocal(r, z).then_inc(z_lin, 2)
                else:
                    dve.wait_ge(z_lin, 3 * n + 3)
                    if L or not isinstance(c, int):
                        dve.wait_ge(raw_used, n)
                    v.tensor_tensor(rz[:, :], r, scale, ALU.mult).then_inc(rz_ready, 1)

            def residual(c):
                dve.wait_ge(rz_ready, NC + c + 1)
                for t in range(CT):
                    xt = xr[:, bass.ds(c * CT + t, 1), :].rearrange("p o f -> p (o f)")
                    last = v.scalar_tensor_tensor(xt, raw[:, t, 0:D], rz[:, t:t + 1], xt, ALU.mult, ALU.add)
                last.then_inc(raw_used, 1)

            def statistics(c):
                for t in range(CT):
                    last = v.bn_stats(bn6c[:, t, :], xr[:, bass.ds(c * CT + t, 1), :].rearrange("p o f -> p (o f)"))
                last.then_inc(ln_lin, 1)

            def aggregate():
                for t in range(CT):
                    last = v.bn_aggr(mvc[:, t, :], bn6c[:, t, :])
                last.then_inc(ln_stats, 1)

            def rest_steps(L, c):
                with dve.If(dve.value_load(general[0:1, 0:1], min_val=0, max_val=1)):
                    with dve.Fori(0, T) as s:
                        dve.wait_ge(rest_e, step_no(L, c, s) + 1)
                        v.tensor_tensor(ringB[RING - 1], ringA[RING - 1], ringB[RING - 1], ALU.max).then_inc(rest_mx, 1)
                        dve.wait_ge(rest_mx, step_no(L, c, s) + 1)
                        dve.wait_ge(rest_in, 16 * (step_no(L, c, s) + 1))
                        v.scalar_tensor_tensor(ringA[RING - 1], ringB[RING - 1], 2.0, rest_sb, ALU.min,
                                               ALU.mult).then_inc(rest_p, 1)

            def chunk(L, c, first, last_chunk, two_exps):
                k = VEC_TOPS if first else 0
                if two_exps:
                    for i in range(k, T):
                        top_step(L, c, i)
                    for part in range(4):
                        maxima(L, c, first, part)
                    row_columns(L, c, first, True)
                for s in range(T):
                    n = step_no(L, c, s)
                    A, B = ringA[s % RING], ringB[s % RING]
                    counts = C4[:, bass.ds(c * CW, CW), s, :]
                    if not first and s == STATS[0] and L == 1:
                        dve.wait_ge(raw_used, NC + c)
                        dve.wait_ge(ln_ready, c)
                    if not first and s == STATS[1] and L == 1:
                        dve.wait_ge(ln_lin, c + 1)
                    mine = s not in POOL_S
                    if two_exps:
                        dve.wait_ge(e_ready if mine else e_pool[L],
                                    dve_no(L, c, s) + 1 if mine else pool_no(0, c, s) + 1)
                        v.tensor_tensor(B, A, B, ALU.max).then_inc(mx_done[L], 1)
                        dve.wait_ge(mx_done[L], c * T + s + 1)
                        if mine:
                            v.scalar_tensor_tensor(A.rearrange("p (w q) -> p w q", q=WQ),
                                                   B.rearrange("p (w q) -> p w q", q=WQ), 2.0, counts,
                                                   ALU.min, ALU.mult).then_inc(p_ready, 1)
                        else:
                            v.tensor_scalar(A, B, 2.0, None, ALU.min).then_inc(x_ready, 1)
                    elif mine:
                        dve.wait_ge(e_ready, dve_no(L, c, s) + 1)
                        A3 = A.rearrange("p (w q) -> p w q", q=WQ)
                        v.scalar_tensor_tensor(A3, A3, floor[:, s:s + 1], counts, ALU.max,
                                               ALU.mult).then_inc(p_ready, 1)
                    if not two_exps:
                        lead = 0 if first else TOPS_FROM
                        k0 = VEC_TOPS if first else 0
                        while k < T and lead + (k - k0) * (T - lead) // (T - k0) <= s:
                            top_step(L, c, k)
                            k += 1
                        if not first and s in CHAIN_AT:
                            maxima(L, c - 1, False, CHAIN_AT.index(s))
                        if s == ROW_AT and not last_chunk:
                            row_columns(L, c + 1, False, False)
                    if not first and s in Z_AT:
                        sums_inverse(L, c - 1, Z_AT.index(s))
                    if not first and L == 1:
                        if s == RESIDUAL_AT:
                            residual(c - 1)
                        if s == STATS[0]:
                            statistics(c - 1)
                        if s == STATS[1]:
                            aggregate()
                    if s == RING - 1 and two_exps:
                        rest_steps(L, c)

            def layer(L, two_exps):
                if not two_exps:
                    dve.wait_ge(fast_ready, L + 1)
                    row_columns(L, 0, True, False)
                chunk(L, 0, True, False, two_exps)
                with dve.Fori(1, NC - 1) as c:
                    chunk(L, c, False, False, two_exps)
                chunk(L, NC - 1, False, True, two_exps)
                if not two_exps:
                    for part in range(4):
                        maxima(L, NC - 1, False, part)

            for L in range(LAYERS):
                scalars(L)
                for k in range(VEC_TOPS):
                    top_step(L, 0, k)
                    layer_vectors(L, k)
                dve.wait_ge(mode_ready, L + 1)
                dve.wait_ge(floor_ready, L + 1)
                with dve.If(dve.value_load(careful[0:1, 0:1], min_val=0, max_val=1)):
                    layer(L, True)
                with dve.Else():
                    layer(L, False)
                for part in range(3):
                    sums_inverse(L, NC - 1, part)
                if L == 1:
                    residual(NC - 1)
                    dve.wait_ge(raw_used, 2 * NC)
                    dve.wait_ge(ln_ready, NC)
                    statistics(NC - 1)
                    dve.wait_ge(ln_lin, NC + 1)
                    aggregate()

        @block.scalar
        def _(act):
            a_ = nc.scalar
            act.wait_ge(prep_T, 1)
            a_.activation(w1T[:, :, :], ps[:, PREP:PREP + KH * 128].rearrange("p (k f) -> p k f", k=KH), ACT.Copy)
            a_.activation(w2T[:, :, :], ps[:, PREP + 256:PREP + 512].rearrange("p (k f) -> p k f", k=KH), ACT.Copy)
            a_.activation(w3T[:, :], ps[:, PREP + 512:PREP + 640], ACT.Copy).then_inc(prep_sb, 1)
            act.wait_ge(prep_v, 1)
            a_.activation(w1v[:, :], ps[:, VEC:VEC + 2], ACT.Copy)
            for k in range(KH):
                a_.activation(w2[:, k, D:AW], ps[:, VEC + 2 + 2 * k:VEC + 4 + 2 * k], ACT.Copy)
            a_.activation(w3[:, D:AW], ps[:, VEC + 6:VEC + 8], ACT.Copy).then_inc(prep_done, 1)
            act.wait_ge(before_sum, 1)
            act.wait_ge(ln_ready, 1)
            for t in range(T):
                last = a_.activation(hA[:, t, 0:D], xr[:, t, :], ACT.Relu, bias=nbias[:, t:t + 1],
                                     scale=rstd[:, t:t + 1])
            last.then_inc(g0_ready, 1)
            act.wait_ge(keys_T, 1)
            for k in range(KC):
                a_.activation(key_lo[:, :, k].rearrange("p (g w) -> p g w", g=WG),
                              tiles(128 * WG * k, WG, rows=128), ACT.Copy)
            for k in range(KC):
                last = a_.activation(key_col[:, :, k].rearrange("p (g w) -> p g w", g=WG),
                                     tiles(128 * WG * (KC + k), WG, rows=128), ACT.Copy, bias=-1.0)
            last.then_inc(keys_sb, 1)
            for c in range(NC):
                with act.Fori(c * CT, (c + 1) * CT) as t:
                    for i, (w0, w1_, at_) in enumerate(HALF):
                        act.wait_ge(half_ok[i], t + 1)
                        a_.activation(C[:, bass.ds((t * TW + w0) * WC, (w1_ - w0) * WC)].rearrange(
                            "p (w c) -> p w c", c=WC), tiles(at_, w1_ - w0), ACT.Copy).then_inc(half_out[i], 1)
                act.wait_ge(g0_T, c + 1)
                if c:
                    act.wait_ge(ab0_ps, c)
                a_.activation(featT0[:, 0:4 * P].rearrange("p (t n) -> p t n", n=P), tiles(G0T[0], 4, rows=D), ACT.Copy)
                a_.activation(featT0[:, 4 * P:CT * P], ps[0:D, G0T[4]:G0T[4] + P], ACT.Copy).then_inc(g0_sb, 1)
            act.wait_ge(ab0_ps, NC)
            a_.activation(ab[0][:, :, :], ps[0:P, AB0:AB0 + 2 * T].rearrange("p (t i) -> p t i", i=2),
                          ACT.Copy).then_inc(ab_ready, 1)

            def exps(A, B, a, al, out_sem):
                a_.activation(A.rearrange("p (t n) -> p t n", n=P), tiles(ROWU), ACT.Exp, bias=a)
                a_.activation(B.rearrange("p (t n) -> p t n", n=P), tiles(ROWV), ACT.Exp,
                              bias=al).then_inc(out_sem, 1)

            def rest_steps(L, c):
                act.wait_ge(flag_ok, 1)
                with act.If(act.value_load(general[0:1, 0:1], min_val=0, max_val=1)):
                    act.wait_ge(pe_done, step_no(L, c, RING))
                    with act.Fori(0, T) as s:
                        act.wait_ge(rest_pe, step_no(L, c, s))
                        one = bass.ds(s, 1)
                        exps(ringA[RING - 1], ringB[RING - 1], ab[L][:, one, 0], a_leak[:, one], rest_e)

            def move_sums(L, c):
                n = L * NC + c
                act.wait_ge(pe_done, step_no(L, c, T))
                act.wait_ge(raw_used, n)
                for i, (t0, t1) in enumerate(((0, 3), (3, CT))):
                    last = a_.activation(raw[:, t0:t1, :], acc3[i], ACT.Copy)
                last.then_inc(raw_ready, 1)

            def factors(L, c):
                act.wait_ge(back_ready, L * NC + c + 1)
                a_.activation(kappa[:, bass.ds(c * CT, CT)], back[:, :], ACT.Exp).then_inc(kappa_ready, 1)

            def copy_featT(L, c):
                act.wait_ge(feat_T, L * NC + c + 1)
                a_.activation(featT.rearrange("p (t n) -> p t n", n=P), tiles(WORK, rows=D),
                              ACT.Copy).then_inc(feat_sb, 1)

            def hidden(c):
                act.wait_ge(h1_ps, c + 1)
                for k in range(KH):
                    last = a_.activation(h1T[:, k, :].rearrange("p (t n) -> p t n", n=P),
                                         tiles(WORK + 128 * CT * k, rows=128), ACT.Relu, bias=b1c[:, k:k + 1])
                last.then_inc(h1_sb, 1)

            def new_features(L, c):
                act.wait_ge(new_ps, L * NC + c + 1)
                if L == 0:
                    act.wait_ge(ones_col, 1)
                for i, (t0, t1) in enumerate(((0, 3), (3, CT))):
                    tc = bass.ds(c * CT + t0, t1 - t0)
                    a_.activation(new_of[L][:, tc, 0:D], new3[i][:, :, 0:D], ACT.Copy)
                    last = a_.activation(ab[L + 1][:, tc, :], new3[i][:, :, D:AW], ACT.Copy)
                last.then_inc(new_sb, 1)

            def normalise(c):
                act.wait_ge(ln_ready, c + 2)
                act.wait_ge(feat_T, NC + c)
                for t in range(CT):
                    one = bass.ds(c * CT + t, 1)
                    last = a_.activation(gn[:, t, :], xr[:, one, :].rearrange("p o f -> p (o f)"), ACT.Relu,
                                         bias=nbias[:, t:t + 1], scale=rstd[:, t:t + 1])
                last.then_inc(g_ready, 1)

            def chunk(L, c, first, two_exps):
                for s in range(T):
                    if s == 0:
                        act.wait_ge(rows_ready, L * NC + c + 1)
                    if not two_exps and s + 1 in POOL_S:
                        a_.activation(ringB[(s + 1) % RING].rearrange("p (t n) -> p t n", n=P), tiles(ROWU), ACT.Relu,
                                      bias=to_relu[:, s + 1:s + 2]).then_inc(relu_done[L], 1)
                    if not (L == 0 and first and s < RING):
                        behind = RING - 2 if two_exps and s == 2 * RING - 1 else RING - 1
                        act.wait_ge(pe_done, step_no(L, c, s) - behind)
                    A = ringA[s % RING]
                    if two_exps:
                        exps(A, ringB[s % RING], ab[L][:, s, 0:1], a_leak[:, s:s + 1],
                             e_pool[L] if s in POOL_S else e_ready)
                    elif s in POOL_S:
                        act.wait_ge(relu_done[L], pool_no(0, c, s) + 1)
                        a_.activation(A, ringB[s % RING], ACT.Exp, bias=to_exp[:, s:s + 1]).then_inc(x_ready, 1)
                    else:
                        a_.activation(A.rearrange("p (t n) -> p t n", n=P), tiles(ROWU), ACT.Exp,
                                      bias=ab[L][:, s, 0:1]).then_inc(e_ready, 1)
                    if s == 0 and two_exps:
                        factors(L, c)
                    if s == KAPPA_AT and not two_exps and not first:
                        factors(L, c - 1)
                    if not first:
                        if s == RING - 2:
                            move_sums(L, c - 1)
                        if s == POST_ACT[L][0]:
                            if L == 1:
                                normalise(c - 1)
                            if L == 0:
                                copy_featT(L, c - 1)
                        if s == POST_ACT[L][1]:
                            if L == 0:
                                hidden(c - 1)
                            if L == 1:
                                copy_featT(L, c - 1)
                        if s == POST_ACT[L][2]:
                            new_features(L, c - 1)
                    if s == RING - 1 and two_exps:
                        rest_steps(L, c)

            def layer(L, two_exps):
                chunk(L, 0, True, two_exps)
                with act.Fori(1, NC) as c:
                    chunk(L, c, False, two_exps)
                move_sums(L, NC - 1)
                if not two_exps:
                    factors(L, NC - 1)

            for L in range(LAYERS):
                act.wait_ge(shift_ready, L + 1)
                a_.activation(floor[:, :], ab[L][:, :, 0], ACT.Exp, bias=shift[:, :],
                              scale=SLOPE).then_inc(floor_ready, 1)
                act.wait_ge(counts_done, 1)
                act.wait_ge(fast_ready, L + 1)
                act.wait_ge(mode_ready, L + 1)
                with act.If(act.value_load(careful[0:1, 0:1], min_val=0, max_val=1)):
                    layer(L, True)
                with act.Else():
                    layer(L, False)
                if L == 0:
                    copy_featT(L, NC - 1)
                    hidden(NC - 1)
                if L == 1:
                    normalise(NC - 1)
                    copy_featT(L, NC - 1)
                if L < 2:
                    new_features(L, NC - 1)
                    act.wait_ge(new_sb, (L + 1) * NC)
                    act.sem_inc(ab_ready, 1)

        @block.tensor
        def _(pe):
            mm, tr = nc.tensor.matmul, nc.tensor.transpose
            pe.wait_ge(dve_consts, 1)
            for k in range(NS):
                pe.wait_ge(before_ok, k + 1)
                for g in range(WG):
                    last = mm(ps[0:P, CNT + g:CNT + g + 1], before[:, k, P * g:P * (g + 1)], ones_b[:, :],
                              start=(k == 0 and g == 0), stop=(k == NS - 1), skip_group_check=True)
            last.then_inc(before_sum, 1)
            pe.wait_ge(weights_in, 16 * N_WEIGHTS)
            pe.wait_ge(consts, N_CONSTS)
            for k in range(KH):
                tr(ps[:, PREP + 128 * k:PREP + 128 * (k + 1)], w1[:, 128 * k:128 * (k + 1)], ident[:, :])
            for k in range(KH):
                tr(ps[:, PREP + 256 + 128 * k:PREP + 384 + 128 * k], w2[:, k, 0:D], ident[:, :])
            tr(ps[:, PREP + 512:PREP + 640], w3[:, 0:D], ident[:, :]).then_inc(prep_T, 1)
            pe.wait_ge(prep_sb, 1)
            for k in range(KH):
                mm(ps[:, VEC:VEC + 2], w1T[:, k, :], av1[:, k, :], start=(k == 0), stop=(k == KH - 1))
            for k in range(KH):
                mm(ps[:, VEC + 2 + 2 * k:VEC + 4 + 2 * k], w2T[:, k, :], av2[:, :], start=True, stop=True)
            mm(ps[:, VEC + 6:VEC + 8], w3T[:, :], av3[:, :], start=True, stop=True).then_inc(prep_v, 1)
            pe.wait_ge(prep_done, 1)
            pe.wait_ge(keys_ok, 2)
            for i, key in enumerate((k_lo, k_hi)):
                for k in range(KC):
                    for g in range(WG):
                        n = 128 * (WG * (KC * i + k) + g)
                        last = tr(ps[0:128, n:n + P], key[:, g, 128 * k:128 * (k + 1)], ident[0:P, 0:P])
            last.then_inc(keys_T, 1)
            mm(ps[0:P, COV:COV + 1], ones_f[:, :], covered[:, :], start=True, stop=True).then_inc(covered_sum, 1)

            def count(t, i):
                pe.wait_ge(hots_ok, t + 1)
                for j, (w0, w1_, at_) in enumerate(HALF):
                    pe.wait_ge(half_out[j], t)
                    for w in range(w0, w1_):
                        o = at_ + 128 * (w - w0)
                        for k in range(KC):
                            last = mm(ps[0:P, o:o + WC], hot_lo[i][:, :, KC * w + k], hot_col[i][:, :, KC * w + k],
                                      start=(k == 0), stop=(k == KC - 1))
                    last.then_inc(half_ok[j], 1)

            def attention_terms(c):
                for t in range(CT):
                    n = AB0 + 2 * (c * CT + t)
                    last = mm(ps[0:P, n:n + 2], featT0[:, P * t:P * (t + 1)], w1v[:, :], start=True, stop=True)
                last.then_inc(ab0_ps, 1)

            pe.wait_ge(keys_sb, 1)
            pe.wait_ge(g0_ready, 1)
            for c in range(NC):
                with pe.Fori(c * CT, (c + 1) * CT - 1, 2) as t:
                    count(t, c % 2)
                    count(t + 1, 1 - c % 2)
                count((c + 1) * CT - 1, c % 2)
                pe.wait_ge(half_out[0], (c + 1) * CT)
                for t in range(CT):
                    last = tr(ps[0:D, G0T[t]:G0T[t] + P], hA[:, c * CT + t, 0:D], ident[0:P, 0:P])
                last.then_inc(g0_T, 1)
                pe.wait_ge(g0_sb, c + 1)
                attention_terms(c)

            pe.wait_ge(flag_ok, 1)
            with pe.If(pe.value_load(general[0:1, 0:1], min_val=0, max_val=1)):
                HAND = EX // U
                pe.wait_ge(half_out[0], T)
                pe.wait_ge(half_out[1], T)
                with pe.Fori(0, P) as b:
                    pe.wait_ge(gen_out, b)
                    mm(ps[0:P, 0:512], zeros[:, 0:P], zeros[:, 0:512], start=True, stop=False)
                    mm(ps[0:P, 512:512 + P], zeros[:, 0:P], zeros[:, 0:P], start=True, stop=False)
                    with pe.Fori(0, HAND) as i:
                        pe.wait_ge(gen_hots, b * HAND + i + 1)
                        for u in range(U):
                            for w in range(WQ):
                                last = mm(ps[0:P, 128 * w:128 * w + WC], g_hot[:, u, 0, :], g_hot[:, u, 1 + w, :],
                                          start=False, stop=False, skip_group_check=True)
                        last.then_inc(gen_mm, 1)
                    mm(ps[0:P, 0:512], zeros[:, 0:P], zeros[:, 0:512], start=False, stop=True)
                    mm(ps[0:P, 512:512 + P], zeros[:, 0:P], zeros[:, 0:P], start=False,
                       stop=True).then_inc(gen_sum, 1)

            def top_transpose(L, c, first):
                n = L * NC + c
                pe.wait_ge(top_done, step_no(L, c, T))
                if not (L == 0 and first):
                    pe.wait_ge(top_max, n)
                for t in range(CT):
                    last = tr(ps[0:P, WORK + 128 * t:WORK + 128 * t + P], top_a[:, P * t:P * (t + 1)],
                              ident[0:P, 0:P])
                last.then_inc(top_T, 1)

            def rows(L, c, first, two_exps):
                n = L * NC + c
                pe.wait_ge(uv_ready, n + 1)
                if not (L == 0 and first):
                    pe.wait_ge(e_ready, dve_no(L, c, 0))
                for i, at_ in enumerate((ROWU, ROWV) if two_exps else (ROWU,)):
                    for t in range(CT):
                        last = tr(ps[0:P, at_ + 128 * t:at_ + 128 * t + P],
                                  uv[:, i, t:t + 1].broadcast_to([P, P]), ident[0:P, 0:P])
                last.then_inc(rows_ready, 1)

            def products(L, A, feat, out_sem, last_of_group):
                for t in range(CT):
                    last = mm(ps[0:P, acc_at(t):acc_at(t) + HW], A[:, P * t:P * (t + 1)], feat,
                              start=False, stop=last_of_group, skip_group_check=last_of_group and t not in (2, CT - 1))
                last.then_inc(out_sem, 1)

            def rest_steps(L, c):
                with pe.If(pe.value_load(general[0:1, 0:1], min_val=0, max_val=1)):
                    with pe.Fori(0, T) as s:
                        pe.wait_ge(rest_p, step_no(L, c, s) + 1)
                        products(L, ringA[RING - 1], h_of[L][:, bass.ds(s, 1), :].rearrange("p o f -> p (o f)"),
                                 rest_pe, False)

            def feat_transposes(L, c, source, ready, n, maxima_of):
                pe.wait_ge(ready, n)
                pe.wait_ge(top_max, L * NC + maxima_of + 1)
                for t in range(CT):
                    last = tr(ps[0:D, WORK + 128 * t:WORK + 128 * t + P], source[:, t, :], ident[0:P, 0:P])
                last.then_inc(feat_T, 1)

            def hidden(c):
                pe.wait_ge(feat_sb, c + 1)
                for k in range(KH):
                    for t in range(CT):
                        o = WORK + 128 * (CT * k + t)
                        last = mm(ps[:, o:o + P], w1[:, 128 * k:128 * (k + 1)], featT[:, P * t:P * (t + 1)],
                                  start=True, stop=True)
                last.then_inc(h1_ps, 1)

            def new_features(L, c):
                if L == 0:
                    pe.wait_ge(h1_sb, c + 1)
                else:
                    pe.wait_ge(feat_sb, NC + c + 1)
                for t in range(CT):
                    o = ps[0:P, new_at(t):new_at(t) + AW]
                    if L == 0:
                        for k in range(KH):
                            last = mm(o, h1T[:, k, P * t:P * (t + 1)], w2[:, k, :], start=(k == 0),
                                      stop=(k == KH - 1))
                    else:
                        last = mm(o, featT[:, P * t:P * (t + 1)], w3[:, :], start=True, stop=True)
                last.then_inc(new_ps, 1)

            def chunk(L, c, first, last_chunk, two_exps):
                if two_exps:
                    if not (L == 0 and first):
                        pe.wait_ge(e_ready, dve_no(L, c, 0))
                    top_transpose(L, c, first)
                    rows(L, c, first, True)
                if not (L == 0 and first):
                    pe.wait_ge(raw_ready, L * NC + c)
                for at_, n in ((0, 3 * HW), (512, 2 * HW)):
                    mm(ps[0:P, at_:at_ + n], zeros[:, 0:P], zeros[:, 0:n], start=True, stop=False)
                for s in range(T):
                    if s in POOL_S:
                        pe.wait_ge(q_ready, pool_no(L, c, s) + 1)
                    else:
                        pe.wait_ge(p_ready, dve_no(L, c, s) + 1)
                    products(L, ringA[s % RING], h_of[L][:, s, :], pe_done, s == T - 1)
                    if s == RING - 1 and two_exps:
                        rest_steps(L, c)
                    if not first:
                        if L == 0 and s == POST_PE[L][0]:
                            feat_transposes(L, c - 1, agg, raw_used, c, c if two_exps else c - 1)
                        if L == 0 and s == POST_PE[L][1]:
                            hidden(c - 1)
                        if L == 1 and s == POST_PE[L][0]:
                            feat_transposes(L, c - 1, gn, g_ready, c, c if two_exps else c - 1)
                        if L < 2 and s == POST_PE[L][2]:
                            new_features(L, c - 1)
                    if s == ROWS_PE and not last_chunk and not two_exps:
                        rows(L, c + 1, False, False)
                if not two_exps:
                    if L < 2 and not first:
                        pe.wait_ge(new_sb, L * NC + c)
                    top_transpose(L, c, first)

            def layer(L, two_exps):
                if not two_exps:
                    rows(L, 0, True, False)
                chunk(L, 0, True, False, two_exps)
                with pe.Fori(1, NC - 1) as c:
                    chunk(L, c, False, False, two_exps)
                chunk(L, NC - 1, False, True, two_exps)

            for L in range(LAYERS):
                if L:
                    pe.wait_ge(new_sb, L * NC)
                pe.wait_ge(mode_ready, L + 1)
                with pe.If(pe.value_load(careful[0:1, 0:1], min_val=0, max_val=1)):
                    layer(L, True)
                with pe.Else():
                    layer(L, False)
                if L == 0:
                    feat_transposes(L, NC - 1, agg, raw_used, NC, NC - 1)
                    hidden(NC - 1)
                if L == 1:
                    feat_transposes(L, NC - 1, gn, g_ready, NC, NC - 1)
                if L < 2:
                    new_features(L, NC - 1)


def kernel(**inputs):
    import numpy as np
    import concourse.bacc as bacc
    from concourse import mybir as mb
    from concourse.bass_utils import run_bass_kernel_spmd

    arrays = {
        "x": inputs["x"],
        "edges": np.stack([inputs["src"], inputs["dst"]], axis=1),
        "W1": inputs["L0_gnn_W1"], "a_src1": inputs["L0_gnn_a_src1"], "a_dst1": inputs["L0_gnn_a_dst1"],
        "b1": inputs["L0_gnn_b1"],
        "W2": inputs["L0_gnn_W2"], "a_src2": inputs["L0_gnn_a_src2"], "a_dst2": inputs["L0_gnn_a_dst2"],
        "b2": inputs["L0_gnn_b2"],
        "W3": inputs["L1_gnn_W"], "a_src3": inputs["L1_gnn_att_src"], "a_dst3": inputs["L1_gnn_att_dst"],
        "b3": inputs["L1_gnn_bias"],
    }
    arrays = {n: np.ascontiguousarray(a) for n, a in arrays.items()}
    nc = bacc.Bacc("TRN2", target_bir_lowering=False, num_devices=1)
    aps = {n: nc.dram_tensor("in_" + n, a.shape, mb.dt.from_np(a.dtype), kind="ExternalInput").ap()
           for n, a in arrays.items()}
    out = nc.dram_tensor("out", inputs["x"].shape, mb.dt.float32, kind="ExternalOutput").ap()
    gat_stack_kernel(nc, out=out, **aps)
    r = run_bass_kernel_spmd(nc, [{"in_" + n: a for n, a in arrays.items()}], core_ids=[0])
    return r.results[0]["out"]
```

```python
from contextlib import ExitStack

import concourse.bass as bass
from concourse import mybir


def gat_stack_kernel(nc, x, edges, W1, a_src1, a_dst1, b1, W2, a_src2, a_dst2, b2,
                     W3, a_src3, a_dst3, b3, out):
    fp32, bf16 = mybir.dt.float32, mybir.dt.bfloat16
    i32, u8 = mybir.dt.int32, mybir.dt.uint8
    ALU, ACT, AX = mybir.AluOpType, mybir.ActivationFunctionType, mybir.AxisListType
    MAX_OVER_PARTITIONS = bass.bass_isa.ReduceOp.max

    N, D = x.shape
    E = edges.shape[0]
    H1 = W1.shape[1]
    KH = H1 // 128
    P = 125
    T = N // P
    WQ = 5
    NW = N // WQ
    WC = T * WQ
    WG = NW // P
    TW = P // WQ
    SLOTS = 256
    REAL = SLOTS - WQ
    KC = SLOTS // 128
    EP = E // P
    SAMPLE = 33
    NS = EP // SAMPLE
    CAP = 254
    CT = 5
    NC = T // CT
    CD = CT * P
    CW = CD // WQ
    RING = 8
    LEAD = 5
    HW = D + 1
    AW = D + 2
    EX = EP + T
    U = 10
    EPS, SLOPE = 1e-5, 0.2
    SPAN_LIMIT = 110.0
    MAGIC = 12582912.0
    assert T * P == N and NW * WQ == N and WG * P == NW and EP * P == E and NS * SAMPLE == EP
    assert EX % U == 0 and WC == P

    x_v = x.rearrange("(t p) f -> p t f", p=P)
    out_v = out.rearrange("(t p) f -> p t f", p=P)
    rest_d = nc.dram_tensor("count_rest", (P, T, N), fp32).ap()

    ctx = ExitStack()
    with ctx:
        def sb(name, shape, dt=fp32):
            return ctx.enter_context(nc.sbuf_tensor(name, shape, dt))

        def sem(name):
            return ctx.enter_context(nc.semaphore(name))

        C = sb("C", [P, NW * WC], u8)
        C4 = C[:, :].rearrange("p (w t q) -> p w t q", t=T, q=WQ)
        xr = sb("xr", [P, T, D])
        hA = sb("hA", [P, T, HW])
        hB = sb("hB", [128, T * HW])
        hB3 = hB[0:P, :].rearrange("p (t f) -> p t f", f=HW)
        iota_t = hB[:, 0:P * TW * KC // 2].bitcast(bf16).rearrange("p (c n) -> p c n", c=P)
        scratch = sb("scratch", [128, 2 * P * TW * KC])
        edge_sb = sb("edge_sb", [P, EP, 2], i32)
        gathered = sb("gathered", [P, WG, SLOTS * 2], i32)
        gath4 = gathered[:, :, :].rearrange("p g (e c) -> p g e c", c=2)
        key_lo = sb("key_lo", [128, NW, KC], bf16)
        key_col = sb("key_col", [128, NW, KC], bf16)
        ident = sb("ident", [128, 128])
        w1 = sb("w1", [D, H1])
        w1T = sb("w1T", [128, KH, D])
        w1v = sb("w1v", [D, 2])
        w2 = sb("w2", [128, KH, AW])
        w2T = sb("w2T", [D, KH, 128])
        w3 = sb("w3", [D, AW])
        w3T = sb("w3T", [D, D])
        av1 = sb("av1", [128, KH, 2])
        av2 = sb("av2", [D, 2])
        av3 = sb("av3", [D, 2])
        b1c = sb("b1c", [128, KH])
        b2r = sb("b2r", [P, D])
        b3r = sb("b3r", [P, D])
        zeros = sb("zeros", [P, 512], bf16)
        ones_b = sb("ones_b", [P, 1], bf16)
        ones_f = sb("ones_f", [P, P])
        sampled = sb("sampled", [P, NS])
        win_base = sb("win_base", [P, WG])
        start_f = sb("start_f", [P, WG])
        start_i = sb("start_i", [P, WG], i32)
        covered = sb("covered", [P, 1])
        covers = sb("covers", [P, 1])
        general = sb("general", [1, 1], i32)
        careful = sb("careful", [1, 1], i32)
        bn6 = sb("bn6", [P, T, 6])
        mv = sb("mv", [P, T, 2])
        bn6c = sb("bn6c", [P, CT, 6])
        mvc = sb("mvc", [P, CT, 2])
        rstd = sb("rstd", [P, T])
        nbias = sb("nbias", [P, T])
        numbers = sb("numbers", [P, P])
        neghalf = sb("neghalf", [P, T])
        ab = [sb(f"ab{L}", [P, T, 2]) for L in range(3)]
        ext = sb("ext", [P, 2])
        extg = sb("extg", [P, 2])
        span = sb("span", [P, 3])
        a_unit = sb("a_unit", [P, T])
        a_neg = sb("a_neg", [P, T])
        a_leak = sb("a_leak", [P, T])
        b_low = sb("b_low", [P, T])
        a_top = sb("a_top", [P, 1])
        is_fast = sb("is_fast", [P, 2])
        b_cut = sb("b_cut", [P, T])
        b_rest = sb("b_rest", [P, T])
        shift = sb("shift", [P, 1])
        floor = sb("floor", [P, T])
        to_relu = sb("to_relu", [P, T])
        to_exp = sb("to_exp", [P, T])
        row_fast = sb("row_fast", [P, T])
        back_fast = sb("back_fast", [P, T])
        mu = sb("mu", [P, CT])
        e_top = sb("e_top", [P, CT])
        m_top = sb("m_top", [P, CT])
        uv = sb("uv", [P, 2, CT])
        back = sb("back", [P, CT])
        kappa = sb("kappa", [P, T])
        zk = sb("zk", [P, 3, CT])
        rz = sb("rz", [P, CT])
        featT0 = sb("featT0", [D, CT * P])

        sc_b = scratch[:, :].bitcast(bf16)
        win_dst = hA[:, :, :].rearrange("p t f -> p (t f)")[:, 0:NW]
        before = sc_b[0:P, 0:NS * NW].rearrange("p (k w) -> p k w", k=NS)
        NSL = WG * SLOTS

        OH = P * TW * KC

        def slot_plane(at):
            return scratch[0:P, at:at + NSL].rearrange("p (g e) -> p g e", g=WG)

        k_hi, k_lo, k_dl, k_ok = (slot_plane(OH + i * NSL) for i in range(4))
        k_in = slot_plane(0)
        hot_lo = [sc_b[:, 2 * i * OH:(2 * i + 1) * OH].rearrange("p (c n) -> p c n", c=P) for i in range(2)]
        hot_col = [sc_b[:, (2 * i + 1) * OH:(2 * i + 2) * OH].rearrange("p (c n) -> p c n", c=P) for i in range(2)]
        g_lo, g_col, g_hi, g_dst, g_win, g_shift = (scratch[0:P, i * EX:(i + 1) * EX] for i in range(6))
        g_at = 6 * EX
        g_iota = scratch[0:P, g_at:g_at + WQ * WC]
        g_plane = scratch[0:P, g_at + 640:g_at + 640 + WQ * WC]
        g_hot = scratch[0:P, g_at + 1280:g_at + 1280 + U * 3 * P].bitcast(bf16).rearrange(
            "p (u k c) -> p u k c", u=U, k=6)
        assert T % RING == 1
        ring = [scratch[0:P, i * CD:(i + 1) * CD] for i in range(RING + 1)]
        slot = [ring[s % RING if s < T - 1 else RING] for s in range(T)]
        side = scratch[0:P, (RING + 1) * CD:(RING + 2) * CD]
        at = (RING + 2) * CD
        top_a = scratch[0:P, at:at + CD]
        rest_sb = scratch[0:P, at + CD:at + 2 * CD]
        at += 2 * CD
        raw = scratch[0:P, at:at + CT * HW].rearrange("p (t f) -> p t f", f=HW)
        at += CT * HW
        agg = scratch[0:P, at:at + CT * D].rearrange("p (t f) -> p t f", f=D)
        at += CT * D
        agg_flat, gn_flat = scratch[0:P, at - CT * D:at - CT * D + CD], scratch[0:P, at:at + CD]
        gn = scratch[0:P, at:at + CT * D].rearrange("p (t f) -> p t f", f=D)
        at += CT * D
        featT = scratch[0:D, at:at + CD]
        at += CD
        h1T = scratch[:, at:at + KH * CD].rearrange("p (k n) -> p k n", k=KH)
        at += KH * CD
        top_b = scratch[0:P, at:at + CD]
        at += CD
        c_bf = scratch[0:P, at:at + CD // 2 + 1].bitcast(bf16)[:, 0:CD]
        assert at + CD // 2 + 1 <= 2 * OH and g_at + 1280 + U * 3 * P <= 2 * OH and NS * NW <= 4 * OH

        ps = ctx.enter_context(nc.psum_tensor("ps", [128, 8 * 512], fp32))

        def tiles(at, n=CT, width=P, rows=P):
            return ps[0:rows, at:at + 128 * n].rearrange("p (t c) -> p t c", c=128)[:, :, 0:width]

        def acc_at(t):
            return 512 * (t // 3) + HW * (t % 3)

        ROWU, ROWV, WORK = 1024, 1024 + 128 * CT, 2560

        def new_at(t):
            return WORK + 512 * (t // 3) + AW * (t % 3)

        acc3 = [ps[0:P, 0:3 * HW].rearrange("p (t f) -> p t f", f=HW),
                ps[0:P, 512:512 + 2 * HW].rearrange("p (t f) -> p t f", f=HW)]
        new3 = [ps[0:P, WORK:WORK + 3 * AW].rearrange("p (t f) -> p t f", f=AW),
                ps[0:P, WORK + 512:WORK + 512 + 2 * AW].rearrange("p (t f) -> p t f", f=AW)]
        PREP, VEC, AB0, CNT, COV = 2560, 2048, 1792, 3584, 3648
        KEYS = (0, 1536)
        G0T = [3584 + 128 * t for t in range(4)] + [1664]
        HALF = [(0, (TW + 1) // 2, 0), ((TW + 1) // 2, TW, 2048)]

        edges_in = sem("edges_in")
        x_in = sem("x_in")
        weights_in = sem("weights_in")
        consts = sem("consts")
        iota_ready = sem("iota_ready")
        dve_consts = sem("dve_consts")
        samples_ok = sem("samples_ok")
        before_ok = sem("before_ok")
        before_sum = sem("before_sum")
        start_lin = sem("start_lin")
        starts_ok = sem("starts_ok")
        gather_in = sem("gather_in")
        keys_lin = sem("keys_lin")
        keys_ok = sem("keys_ok")
        covered_sum = sem("covered_sum")
        flag_ok = sem("flag_ok")
        keys_T = sem("keys_T")
        keys_sb = sem("keys_sb")
        prep_T = sem("prep_T")
        prep_sb = sem("prep_sb")
        prep_v = sem("prep_v")
        prep_done = sem("prep_done")
        hots_ok = sem("hots_ok")
        half_ok = [sem("half0_ok"), sem("half1_ok")]
        half_out = [sem("half0_out"), sem("half1_out")]
        ones_col = sem("ones_col")
        gen_lin = sem("gen_lin")
        gen_hots = sem("gen_hots")
        gen_mm = sem("gen_mm")
        gen_sum = sem("gen_sum")
        gen_out = sem("gen_out")
        gen_plane = sem("gen_plane")
        gen_stored = sem("gen_stored")
        counts_done = sem("counts_done")
        ln_lin = sem("ln_lin")
        ln_stats = sem("ln_stats")
        ln_pool = sem("ln_pool")
        ln_ready = sem("ln_ready")
        g0_ready = sem("g0_ready")
        g0_T = sem("g0_T")
        g0_sb = sem("g0_sb")
        ab0_ps = sem("ab0_ps")
        ab_ready = sem("ab_ready")
        ext_lin = sem("ext_lin")
        prep_lin = sem("prep_lin")
        shift_ready = sem("shift_ready")
        floor_ready = sem("floor_ready")
        mode_ready = sem("mode_ready")
        fast_ready = sem("fast_ready")
        back_ready = sem("back_ready")
        kappa_ready = sem("kappa_ready")
        raw_ready = sem("raw_ready")
        raw_used = sem("raw_used")
        z_lin = sem("z_lin")
        ext_ready = sem("ext_ready")
        extg_ready = sem("extg_ready")
        scal_lin = sem("scal_lin")
        scal_ready = sem("scal_ready")
        e_ready = sem("e_ready")
        e_pool = [sem(f"e_pool{L}") for L in range(3)]
        relu_done = [sem(f"relu_done{L}") for L in range(3)]
        counts_bf = sem("counts_bf")
        x_ready = sem("x_ready")
        q_ready = sem("q_ready")
        b2_added = sem("b2_added")
        mx_done = [sem(f"mx_done{L}") for L in range(3)]
        p_ready = sem("p_ready")
        pe_done = sem("pe_done")
        top_done = sem("top_done")
        top_T = sem("top_T")
        top_max = sem("top_max")
        m_lin = sem("m_lin")
        uv_ready = sem("uv_ready")
        rows_ready = sem("rows_ready")
        rz_ready = sem("rz_ready")
        feat_T = sem("feat_T")
        feat_sb = sem("feat_sb")
        h1_ps = sem("h1_ps")
        h1_sb = sem("h1_sb")
        new_ps = sem("new_ps")
        new_sb = sem("new_sb")
        res_lin = sem("res_lin")
        g_ready = sem("g_ready")
        y_ready = sem("y_ready")
        out_done = sem("out_done")
        rest_in = sem("rest_in")
        rest_e = sem("rest_e")
        rest_mx = sem("rest_mx")
        rest_p = sem("rest_p")
        rest_pe = sem("rest_pe")

        N_WEIGHTS, N_CONSTS = 15, 7
        VEC_TOPS = 6
        SUMS_AT = 3
        tops = [(top_b, gn_flat), (top_b, agg_flat), (top_b, gn_flat)]
        CHAIN_AT = (2, 3, 4, 5)
        ROW_AT, ROWS_PE = 16, 20
        KAPPA_AT = 8
        Z_AT = (6, 7, 8)
        RESIDUAL_AT, STATS = 8, (9, 10)
        POST_POOL = [((9, 0),), ((11, 3),), ((12, 0), (15, 1), (18, 2))]
        POST_PE = [(9, 12, 15), (13, None, 15), (None, None, None)]
        POST_ACT = [(16, 19, 22), (16, 19, 22), (None, None, None)]
        LAYERS = 3
        h_of = [hA[:, :, :], hB3, hA[:, :, :]]
        new_of = [hB3, hA[:, :, :], None]

        def step_no(L, c, s):
            return (L * NC + c) * T + s

        POOL_S = tuple(range(2, T - 1, 3))

        def pool_before(s):
            return sum(1 for i in POOL_S if i < s)

        def pool_no(L, c, s):
            return (L * NC + c) * len(POOL_S) + pool_before(s)

        def dve_no(L, c, s):
            return (L * NC + c) * (T - len(POOL_S)) + s - pool_before(s)

        block = ctx.enter_context(nc.Block())

        @block.sync
        def _(sp):
            sp.dma_start(edge_sb[:, :, :], edges.rearrange("(p k) c -> p k c", p=P)).then_inc(edges_in, 16)
            sp.dma_start(xr[:, :, :], x_v).then_inc(x_in, 16)
            sp.dma_start(w1[:, :], W1).then_inc(weights_in, 16)
            sp.dma_start(w2[:, :, 0:D], W2.rearrange("(k p) f -> p k f", p=128)).then_inc(weights_in, 16)
            sp.dma_start(w3[:, 0:D], W3).then_inc(weights_in, 16)
            for k in range(KH):
                sp.dma_start(b1c[:, k:k + 1], b1[128 * k:128 * (k + 1)].unsqueeze(1)).then_inc(weights_in, 16)
            for i, a in enumerate((a_src1, a_dst1)):
                for k in range(KH):
                    sp.dma_start(av1[:, k, i:i + 1], a[128 * k:128 * (k + 1)].unsqueeze(1)).then_inc(weights_in, 16)
            for v, pair in ((av2, (a_src2, a_dst2)), (av3, (a_src3, a_dst3))):
                for i, a in enumerate(pair):
                    sp.dma_start(v[:, i:i + 1], a.unsqueeze(1)).then_inc(weights_in, 16)
            sp.dma_start(b2r[:, :], b2.unsqueeze(0).broadcast_to([P, D])).then_inc(weights_in, 16)
            sp.dma_start(b3r[:, :], b3.unsqueeze(0).broadcast_to([P, D])).then_inc(weights_in, 16)

            sp.wait_ge(flag_ok, 1)
            with sp.If(sp.value_load(general[0:1, 0:1], min_val=0, max_val=1)):
                with sp.Fori(0, P) as b:
                    first = sp.snap(b * WQ * WQ)
                    sp.wait_ge(gen_plane, b + 1)
                    sp.dma_start(rest_d[:, :, bass.ds(first, WQ * WQ)],
                                 g_plane.rearrange("p (t d) -> p t d", t=T)).then_inc(gen_stored, 16)

            def rest_loads(L, c):
                with sp.If(sp.value_load(general[0:1, 0:1], min_val=0, max_val=1)):
                    sp.wait_ge(gen_stored, 16 * P + 1)
                    with sp.Fori(0, T) as s:
                        tile, first = sp.snap(s + 0), sp.snap(c * CD)
                        sp.wait_ge(rest_pe, step_no(L, c, s) + 1)
                        sp.wait_ge(counts_done, 1)
                        sp.dma_start(rest_sb, rest_d[:, bass.ds(tile, 1), bass.ds(first, CD)].rearrange(
                            "p t d -> p (t d)")).then_inc(rest_in, 16)

            def store(c):
                sp.wait_ge(y_ready, c + 1)
                sp.dma_start(out_v[:, bass.ds(c * CT, CT), :], xr[:, bass.ds(c * CT, CT), :]).then_inc(out_done, 16)

            for L in range(LAYERS - 1):
                with sp.Fori(0, NC) as c:
                    rest_loads(L, c)
            for c in range(NC):
                rest_loads(LAYERS - 1, c)
                if c:
                    store(c - 1)
            store(NC - 1)
            sp.wait_ge(out_done, 16 * NC)

        @block.gpsimd
        def _(pool):
            g = nc.gpsimd
            g.iota(win_dst, [[WQ, NW]], 0, channel_multiplier=0,
                   allow_small_or_imprecise_dtypes=True).then_inc(consts, 1)
            g.iota(win_base[:, :], [[WQ * P, WG]], 0, channel_multiplier=WQ,
                   allow_small_or_imprecise_dtypes=True).then_inc(consts, 1)
            g.iota(gath4[:, :, REAL:SLOTS, :], [[WQ * P, WG], [1, WQ], [0, 2]], 0,
                   channel_multiplier=WQ).then_inc(consts, 1)
            g.memset(ident[:, :], 1.0).then_inc(consts, 1)
            pool.wait_ge(consts, 4)
            g.affine_select(out=ident[:, :], in_=ident[:, :], compare_op=ALU.is_equal, fill=0.0, base=0,
                            pattern=[[-1, 128]], channel_multiplier=1).then_inc(consts, 1)
            g.memset(neghalf[:, :], -0.5).then_inc(consts, 1)
            g.iota(numbers[:, :], [[1, P]], 0, channel_multiplier=0,
                   allow_small_or_imprecise_dtypes=True).then_inc(consts, 1)
            g.iota(iota_t, [[1, P], [0, TW * KC]], 0, channel_multiplier=0,
                   allow_small_or_imprecise_dtypes=True).then_inc(iota_ready, 1)
            pool.wait_ge(consts, N_CONSTS)
            pool.wait_ge(starts_ok, 1)
            for i in range(WG):
                g.indirect_dma_start(gathered[:, i, 0:2 * REAL], None, edges,
                                     bass.IndirectOffsetOnAxis(ap=start_i[:, i:i + 1], axis=0)
                                     ).then_inc(gather_in, 16)

            def norm_scalars(var, mean, r, nb, half, n):
                g.tensor_scalar(r, var, EPS, None, ALU.add).then_inc(ln_pool, 1)
                pool.wait_ge(ln_pool, n + 1)
                g.tensor_tensor(r, r, half, ALU.pow).then_inc(ln_pool, 1)
                g.tensor_scalar(nb, mean, -1.0, None, ALU.mult).then_inc(ln_pool, 1)
                pool.wait_ge(ln_pool, n + 3)
                g.tensor_tensor(nb, nb, r, ALU.mult).then_inc(ln_ready, 1)

            pool.wait_ge(ln_stats, 1)
            norm_scalars(mv[:, :, 1], mv[:, :, 0], rstd[:, :], nbias[:, :], neghalf[:, :], 0)

            def extremes(L):
                pool.wait_ge(ext_ready, L + 1)
                g.partition_all_reduce(extg[:, :], ext[:, :], P, MAX_OVER_PARTITIONS).then_inc(extg_ready, 1)

            def blocks(L, c, s0, s1):
                for s in POOL_S:
                    if s0 <= s < s1:
                        A = slot[s]
                        pool.wait_ge(counts_bf, pool_no(L, c, s) + 1)
                        pool.wait_ge(x_ready, pool_no(L, c, s) + 1)
                        g.tensor_tensor(A, A, c_bf, ALU.mult).then_inc(q_ready, 1)
                        pool.wait_ge(q_ready, pool_no(L, c, s) + 1)
                        i = POOL_S.index(s) + 1
                        if i < len(POOL_S):
                            widen(c, POOL_S[i])
                        elif L * NC + c + 1 < LAYERS * NC:
                            widen((c + 1) % NC, POOL_S[0])

            def widen(c, s):
                g.tensor_copy(c_bf.rearrange("p (w q) -> p w q", q=WQ),
                              C4[:, c * CW:(c + 1) * CW, s, :]).then_inc(counts_bf, 1)

            def scaled_sums(c):
                pool.wait_ge(rz_ready, c + 1)
                pool.wait_ge(feat_T, c)
                g.tensor_tensor(agg, raw[:, :, 0:D], rz[:, :].unsqueeze(2).broadcast_to([P, CT, D]),
                                ALU.mult).then_inc(raw_used, 1)

            def result(c, part):
                n = (LAYERS - 1) * NC + c
                xc = xr[:, c * CT:(c + 1) * CT, :]
                if part == 0:
                    pool.wait_ge(rz_ready, n + 1)
                    g.tensor_tensor(agg, raw[:, :, 0:D], rz[:, :].unsqueeze(2).broadcast_to([P, CT, D]),
                                    ALU.mult).then_inc(raw_used, 1)
                elif part == 1:
                    pool.wait_ge(raw_used, n + 2)
                    g.tensor_tensor(xc, xc, agg, ALU.add).then_inc(res_lin, 1)
                else:
                    pool.wait_ge(res_lin, c + 1)
                    g.tensor_tensor(xc, xc, b3r[:, :].unsqueeze(1).broadcast_to([P, CT, D]),
                                    ALU.add).then_inc(y_ready, 1)

            def post(L, c, part):
                if L == 0:
                    scaled_sums(c)
                elif L == 2:
                    result(c, part)
                else:
                    pool.wait_ge(ln_stats, c + 2)
                    pool.wait_ge(g_ready, c)
                    norm_scalars(mvc[:, :, 1], mvc[:, :, 0], rstd[:, 0:CT], nbias[:, 0:CT],
                                 neghalf[:, 0:CT], c * 3 + 3)

            pool.wait_ge(weights_in, 16 * N_WEIGHTS)
            pool.wait_ge(g0_ready, 1)
            g.tensor_tensor(xr[:, :, :], xr[:, :, :], b2r[:, :].unsqueeze(1).broadcast_to([P, T, D]),
                            ALU.add).then_inc(b2_added, 1)
            extremes(0)
            pool.wait_ge(hots_ok, T + 1)
            g.memset(hB3[:, :, D:HW], 1.0).then_inc(ones_col, 1)
            pool.wait_ge(b2_added, 1)
            pool.wait_ge(counts_done, 1)
            widen(0, POOL_S[0])
            for L in range(LAYERS):
                if L:
                    extremes(L)
                for c in range(NC):
                    s = 0
                    for at_, part in POST_POOL[L]:
                        blocks(L, c, s, at_)
                        if c:
                            post(L, c - 1, part)
                        s = at_
                    blocks(L, c, s, T)
                for _at, part in POST_POOL[L]:
                    post(L, NC - 1, part)

        @block.vector
        def _(dve):
            v = nc.vector
            v.memset(ones_b[:, :], 1.0)
            v.memset(ones_f[:, :], 1.0)
            v.memset(zeros[:, :], 0.0).then_inc(dve_consts, 1)
            dve.wait_ge(edges_in, 16)
            v.tensor_copy(sampled[:, :], edge_sb[:, :, :].rearrange("p (k r) c -> p k r c", r=SAMPLE)[:, :, 0, 1]
                          ).then_inc(samples_ok, 1)
            dve.wait_ge(samples_ok, 1)
            dve.wait_ge(consts, N_CONSTS)
            for k in range(NS):
                v.tensor_scalar(before[:, k, :], win_dst, sampled[:, k:k + 1], None,
                                ALU.is_gt).then_inc(before_ok, 1)
            dve.wait_ge(before_sum, 1)
            v.tensor_scalar(start_f[:, :], ps[0:P, CNT:CNT + WG], float(SAMPLE), float(1 - SAMPLE),
                            ALU.mult, ALU.add).then_inc(start_lin, 1)
            dve.wait_ge(start_lin, 1)
            v.tensor_scalar(start_i[:, :], start_f[:, :], 0.0, float(E - REAL), ALU.max,
                            ALU.min).then_inc(starts_ok, 1)
            dve.wait_ge(x_in, 16)
            for t in range(T):
                last = v.bn_stats(bn6[:, t, :], xr[:, t, :])
            last.then_inc(ln_lin, 1)
            dve.wait_ge(ln_lin, 1)
            for t in range(T):
                last = v.bn_aggr(mv[:, t, :], bn6[:, t, :])
            last.then_inc(ln_stats, 1)
            v.memset(hA[:, :, D:HW], 1.0).then_inc(dve_consts, 1)
            dve.wait_ge(gather_in, 16 * WG)
            src, dst = gath4[:, :, :, 0], gath4[:, :, :, 1]
            v.tensor_scalar(k_hi, src, 1.0 / P, -0.5 + 0.5 / P, ALU.mult, ALU.add).then_inc(keys_lin, 1)
            v.tensor_tensor(k_dl, dst, win_base[:, :].unsqueeze(2).broadcast_to([P, WG, SLOTS]),
                            ALU.subtract).then_inc(keys_lin, 1)
            dve.wait_ge(keys_lin, 1)
            v.tensor_scalar(k_hi, k_hi, MAGIC, MAGIC, ALU.add, ALU.subtract).then_inc(keys_lin, 1)
            dve.wait_ge(keys_lin, 2)
            v.tensor_scalar(k_in, k_dl, 0.0, None, ALU.is_ge).then_inc(keys_lin, 1)
            dve.wait_ge(keys_lin, 3)
            v.scalar_tensor_tensor(k_lo, k_hi, -float(P), src, ALU.mult, ALU.add).then_inc(keys_ok, 1)
            dve.wait_ge(keys_lin, 4)
            v.scalar_tensor_tensor(k_ok, k_dl, float(WQ - 1), k_in, ALU.is_le, ALU.mult).then_inc(keys_lin, 1)
            dve.wait_ge(keys_ok, 1)
            v.scalar_tensor_tensor(k_hi, k_hi, float(WQ), k_dl, ALU.mult, ALU.add).then_inc(keys_lin, 1)
            dve.wait_ge(keys_lin, 6)
            v.scalar_tensor_tensor(k_hi, k_hi, 1.0, k_ok, ALU.add, ALU.mult).then_inc(keys_ok, 1)
            v.tensor_reduce(covered[:, :], k_ok, AX.XY, ALU.add).then_inc(keys_ok, 1)
            dve.wait_ge(iota_ready, 1)

            def one_hots(t, i, behind, w0=0, w1_=TW):
                if behind:
                    dve.wait_ge(half_ok[1], t - 1)
                for n, (hot, key) in enumerate(((hot_lo[i], key_lo), (hot_col[i], key_col))):
                    if not behind and w0 == 0:
                        dve.wait_ge(keys_sb, n + 1)
                    keys = key[:, bass.ds(t * TW + w0, w1_ - w0), :].rearrange("p w k -> p (w k)")
                    last = v.tensor_tensor(hot[:, :, KC * w0:KC * w1_],
                                           keys.unsqueeze(1).broadcast_to([128, P, KC * (w1_ - w0)]),
                                           iota_t[:, :, KC * w0:KC * w1_], ALU.is_equal)
                last.then_inc(hots_ok, 1)

            one_hots(0, 0, False)
            dve.wait_ge(keys_ok, 3)
            one_hots(1, 1, False)
            dve.wait_ge(covered_sum, 1)
            v.tensor_scalar(covers[:, :], ps[0:P, COV:COV + 1], float(E + N), None, ALU.is_equal)
            v.tensor_scalar(general[0:1, 0:1], ps[0:1, COV:COV + 1], float(E + N), None,
                            ALU.not_equal).then_inc(flag_ok, 1)
            with dve.Fori(2, T - 1, 2) as t:
                one_hots(t, 0, True)
                one_hots(t + 1, 1, True)
            for w0, w1_, _at in HALF:
                one_hots(T - 1, 0, w0 == 0, w0, w1_)

            def scalars(L):
                a, b = ab[L][:, :, 0], ab[L][:, :, 1]
                dve.wait_ge(ab_ready, L + 1)
                v.tensor_scalar(a_neg[:, :], a, -1.0, None, ALU.mult).then_inc(ext_lin, 1)
                v.tensor_reduce(ext[:, 0:1], a, AX.X, ALU.max)
                dve.wait_ge(ext_lin, L + 1)
                v.tensor_reduce(ext[:, 1:2], a_neg[:, :], AX.X, ALU.max).then_inc(ext_ready, 1)
                v.tensor_scalar(a_leak[:, :], a, SLOPE, None, ALU.mult)
                dve.wait_ge(extg_ready, L + 1)
                v.tensor_tensor(span[:, 0:1], extg[:, 0:1], extg[:, 1:2], ALU.add).then_inc(scal_lin, 1)
                v.tensor_scalar(b_low[:, :], b, extg[:, 1:2], None, ALU.subtract)
                dve.wait_ge(scal_lin, 3 * L + 1)
                v.tensor_scalar(span[:, 1:2], span[:, 0:1], 1e-30, None, ALU.max).then_inc(scal_lin, 1)
                dve.wait_ge(scal_lin, 3 * L + 2)
                v.reciprocal(span[:, 2:3], span[:, 1:2]).then_inc(scal_lin, 1)
                dve.wait_ge(scal_lin, 3 * L + 3)
                v.tensor_scalar(a_unit[:, :], a, extg[:, 1:2], span[:, 2:3], ALU.add,
                                ALU.mult).then_inc(scal_ready, 1)
                dve.wait_ge(scal_ready, L + 1)

            def layer_vectors(L, part):
                b = ab[L][:, :, 1]
                if part == 0:
                    v.tensor_scalar(a_top[:, :], extg[:, 0:1], -SLOPE, None, ALU.mult)
                    v.tensor_scalar(is_fast[:, 0:1], span[:, 0:1], SPAN_LIMIT, covers[:, :], ALU.is_le, ALU.mult)
                    v.tensor_scalar(b_cut[:, :], b, extg[:, 1:2], 1.0 - SLOPE, ALU.min,
                                    ALU.mult).then_inc(prep_lin, 1)
                elif part == 1:
                    dve.wait_ge(prep_lin, 2 * L + 1)
                    v.scalar_tensor_tensor(shift[:, :], span[:, 0:1], -(1.0 - SLOPE) / 2, a_top[:, :], ALU.mult,
                                           ALU.add).then_inc(shift_ready, 1)
                    v.tensor_scalar(is_fast[:, 1:2], is_fast[:, 0:1], -1.0, None, ALU.mult)
                    v.tensor_scalar(careful[:, :], is_fast[0:1, 0:1], 0.0, None, ALU.is_equal).then_inc(mode_ready, 1)
                    v.tensor_tensor(b_rest[:, :], b, b_cut[:, :], ALU.subtract).then_inc(prep_lin, 1)
                else:
                    dve.wait_ge(prep_lin, 2 * L + 2)
                    a = ab[L][:, :, 0]
                    v.tensor_scalar(to_relu[:, :], a, 1.0 - SLOPE, shift[:, :], ALU.mult, ALU.subtract)
                    v.tensor_scalar(to_exp[:, :], a, SLOPE, shift[:, :], ALU.mult, ALU.add)
                    v.tensor_scalar(row_fast[:, :], b_cut[:, :], shift[:, :], is_fast[:, 0:1], ALU.add, ALU.mult)
                    v.tensor_scalar(back_fast[:, :], b_rest[:, :], shift[:, :], is_fast[:, 0:1], ALU.subtract,
                                    ALU.mult).then_inc(fast_ready, 1)

            scalars(0)
            for part in range(3):
                layer_vectors(0, part)
            dve.wait_ge(half_out[0], T + 1)
            dve.wait_ge(half_out[1], T + 1)

            dve.wait_ge(flag_ok, 1)
            with dve.If(dve.value_load(general[0:1, 0:1], min_val=0, max_val=1)):
                n = [0]

                def then(ins):
                    n[0] += 1
                    ins.then_inc(gen_lin, 1)
                    dve.wait_ge(gen_lin, n[0])

                then(v.memset(g_win, 0.0))
                then(v.tensor_copy(g_lo[:, 0:EP], edge_sb[:, :, 0]))
                then(v.tensor_copy(g_dst[:, 0:EP], edge_sb[:, :, 1]))
                for t in range(T):
                    then(v.tensor_scalar(g_lo[:, EP + t:EP + t + 1], win_base[:, 0:1], 1.0 / WQ, float(P * t),
                                         ALU.mult, ALU.add))
                then(v.tensor_scalar(g_lo[:, EP:EX], g_lo[:, EP:EX], MAGIC, MAGIC, ALU.add, ALU.subtract))
                then(v.tensor_copy(g_dst[:, EP:EX], g_lo[:, EP:EX]))
                then(v.tensor_scalar(g_hi, g_lo, 1.0 / P, -0.5 + 0.5 / P, ALU.mult, ALU.add))
                then(v.tensor_scalar(g_hi, g_hi, MAGIC, MAGIC, ALU.add, ALU.subtract))
                then(v.scalar_tensor_tensor(g_lo, g_hi, -float(P), g_lo, ALU.mult, ALU.add))
                then(v.tensor_scalar(g_win, g_dst, 1.0 / WQ, -0.5 + 0.5 / WQ, ALU.mult, ALU.add))
                then(v.tensor_scalar(g_win, g_win, MAGIC, MAGIC, ALU.add, ALU.subtract))
                then(v.scalar_tensor_tensor(g_col, g_hi, float(WQ), g_dst, ALU.mult, ALU.add))
                then(v.scalar_tensor_tensor(g_col, g_win, float(WC - WQ), g_col, ALU.mult, ALU.add))
                for w in range(WQ):
                    then(v.tensor_scalar(g_iota[:, WC * w:WC * (w + 1)], numbers[:, :], float(WC * w), None,
                                         ALU.add))
                then(v.tensor_copy(g_shift, g_col))
                HAND = EX // U
                with dve.Fori(0, P) as b:
                    with dve.Fori(0, HAND) as i:
                        dve.wait_ge(gen_mm, b * HAND + i + 1)
                        for u in range(U):
                            e = bass.ds(i * U + u, 1)
                            v.tensor_scalar(g_hot[:, u, 0, :], g_iota[:, 0:P], g_lo[:, e], None, ALU.is_equal)
                            last = v.tensor_scalar(g_hot[:, u, 1:6, :].rearrange("p k c -> p (k c)"), g_iota,
                                                   g_shift[:, e], None, ALU.is_equal)
                        last.then_inc(gen_hots, 1)
                    dve.wait_ge(gen_sum, b + 1)
                    v.tensor_scalar(C[:, bass.ds(b * WQ * WC, WQ * WC)].rearrange("p (w c) -> p w c", w=WQ),
                                    tiles(0, WQ), float(CAP), None, ALU.min)
                    dve.wait_ge(gen_stored, b * 16 + 1)
                    for w in range(WQ):
                        last = v.tensor_scalar(
                            g_plane.rearrange("p (t w q) -> p t w q", t=T, w=WQ)[:, :, w, :],
                            ps[0:P, 128 * w:128 * w + WC].rearrange("p (t q) -> p t q", q=WQ),
                            float(CAP), float(CAP), ALU.max, ALU.subtract)
                    last.then_inc(gen_plane, 1)
                    v.tensor_scalar(g_shift, g_shift, -float(WQ * WC), None, ALU.add).then_inc(gen_out, 1)
                    dve.wait_ge(gen_out, b + 2)
                dve.wait_ge(gen_stored, 16 * P + 1)
            v.memset(rz[:, :], 0.0).then_inc(counts_done, 1)

            def top_step(L, c, s):
                counts = C4[:, bass.ds(c * CW, CW), s, :]
                top = tops[L][s % 2].rearrange("p (w q) -> p w q", q=WQ)
                n = (L * NC + c) * (T + 1)
                if s > 1 or L or not (isinstance(c, int) and c == 0):
                    dve.wait_ge(top_done, n + max(s - 1, 0))
                if s < 2:
                    v.tensor_scalar(top, counts, a_unit[:, s:s + 1], None, ALU.min).then_inc(top_done, 1)
                else:
                    v.scalar_tensor_tensor(top, counts, a_unit[:, s:s + 1], top, ALU.min,
                                           ALU.max).then_inc(top_done, 1)

            def join_tops(L, c):
                dve.wait_ge(top_done, (L * NC + c) * (T + 1) + T)
                if L or not (isinstance(c, int) and c == 0):
                    dve.wait_ge(top_T, L * NC + c)
                v.tensor_tensor(top_a, tops[L][0], tops[L][1], ALU.max).then_inc(top_done, 1)

            def maxima(L, c, first, part):
                n = L * NC + c
                tc = bass.ds(c * CT, CT)
                if part == 0:
                    dve.wait_ge(top_T, n + 1)
                    v.tensor_reduce(mu[:, :], tiles(WORK), AX.X, ALU.max).then_inc(top_max, 1)
                elif part == 1:
                    dve.wait_ge(top_max, n + 1)
                    v.scalar_tensor_tensor(e_top[:, :], mu[:, :], span[:, 1:2], b_low[:, tc], ALU.mult,
                                           ALU.add).then_inc(m_lin, 1)
                elif part == 2:
                    dve.wait_ge(m_lin, 2 * n + 1)
                    v.scalar_tensor_tensor(m_top[:, :], e_top[:, :], SLOPE, e_top[:, :], ALU.mult,
                                           ALU.max).then_inc(m_lin, 1)
                else:
                    dve.wait_ge(m_lin, 2 * n + 2)
                    dve.wait_ge(fast_ready, L + 1)
                    if not (L == 0 and first):
                        dve.wait_ge(kappa_ready, n + 1)
                    v.scalar_tensor_tensor(back[:, :], m_top[:, :], is_fast[:, 1:2], back_fast[:, tc], ALU.mult,
                                           ALU.add).then_inc(back_ready, 1)

            def row_columns(L, c, first, two_exps):
                n = L * NC + c
                tc = bass.ds(c * CT, CT)
                if not (L == 0 and first):
                    dve.wait_ge(rows_ready, n)
                if two_exps:
                    v.tensor_tensor(uv[:, 0, :], ab[L][:, tc, 1], m_top[:, :], ALU.subtract)
                    v.scalar_tensor_tensor(uv[:, 1, :], ab[L][:, tc, 1], SLOPE, m_top[:, :], ALU.mult,
                                           ALU.subtract).then_inc(uv_ready, 1)
                else:
                    v.tensor_copy(uv[:, 0, :], row_fast[:, tc]).then_inc(uv_ready, 1)

            def sums_inverse(L, c, part):
                n = L * NC + c
                z, r = zk[:, 1, :] if L == LAYERS - 1 else zk[:, 0, :], zk[:, 2, :]
                scale = kappa[:, bass.ds(c * CT, CT)]
                if part == 0:
                    dve.wait_ge(raw_ready, n + 1)
                    dve.wait_ge(kappa_ready, n + 2)
                    v.tensor_tensor(zk[:, 0, :], raw[:, :, D], scale, ALU.mult).then_inc(z_lin, 1)
                elif part == 1:
                    dve.wait_ge(z_lin, 3 * n + 1)
                    if L == LAYERS - 1:
                        v.tensor_scalar(z, zk[:, 0, :], 1e-16, None, ALU.add).then_inc(z_lin, 1)
                        dve.wait_ge(z_lin, 3 * n + 2)
                        v.reciprocal(r, z).then_inc(z_lin, 1)
                    else:
                        v.reciprocal(r, z).then_inc(z_lin, 2)
                else:
                    dve.wait_ge(z_lin, 3 * n + 3)
                    if L or not isinstance(c, int):
                        dve.wait_ge(raw_used, n + 1)
                    v.tensor_tensor(rz[:, :], r, scale, ALU.mult).then_inc(rz_ready, 1)

            def residual(c):
                dve.wait_ge(rz_ready, NC + c + 1)
                for t in range(CT):
                    xt = xr[:, bass.ds(c * CT + t, 1), :].rearrange("p o f -> p (o f)")
                    last = v.scalar_tensor_tensor(xt, raw[:, t, 0:D], rz[:, t:t + 1], xt, ALU.mult, ALU.add)
                last.then_inc(raw_used, 1)

            def statistics(c):
                for t in range(CT):
                    last = v.bn_stats(bn6c[:, t, :], xr[:, bass.ds(c * CT + t, 1), :].rearrange("p o f -> p (o f)"))
                last.then_inc(ln_lin, 1)

            def aggregate():
                for t in range(CT):
                    last = v.bn_aggr(mvc[:, t, :], bn6c[:, t, :])
                last.then_inc(ln_stats, 1)

            def rest_steps(L, c):
                with dve.If(dve.value_load(general[0:1, 0:1], min_val=0, max_val=1)):
                    with dve.Fori(0, T) as s:
                        dve.wait_ge(rest_e, step_no(L, c, s) + 1)
                        v.tensor_tensor(top_b, slot[LEAD - 1], top_b, ALU.max).then_inc(rest_mx, 1)
                        dve.wait_ge(rest_mx, step_no(L, c, s) + 1)
                        dve.wait_ge(rest_in, 16 * (step_no(L, c, s) + 1))
                        v.scalar_tensor_tensor(slot[LEAD - 1], top_b, 2.0, rest_sb, ALU.min,
                                               ALU.mult).then_inc(rest_p, 1)

            def chunk(L, c, first, last_chunk, two_exps):
                k = VEC_TOPS if first else 0
                if two_exps:
                    for i in range(k, T):
                        top_step(L, c, i)
                    join_tops(L, c)
                    for part in range(4):
                        maxima(L, c, first, part)
                    row_columns(L, c, first, True)
                for s in range(T):
                    n = step_no(L, c, s)
                    A, B = slot[s], side
                    counts = C4[:, bass.ds(c * CW, CW), s, :]
                    if not first and s == STATS[0] and L == 1:
                        dve.wait_ge(raw_used, NC + c + 1)
                        dve.wait_ge(ln_ready, c)
                    if not first and s == STATS[1] and L == 1:
                        dve.wait_ge(ln_lin, c + 1)
                    mine = s not in POOL_S
                    if two_exps:
                        dve.wait_ge(e_ready if mine else e_pool[L],
                                    dve_no(L, c, s) + 1 if mine else pool_no(0, c, s) + 1)
                        v.tensor_tensor(B, A, B, ALU.max).then_inc(mx_done[L], 1)
                        dve.wait_ge(mx_done[L], c * T + s + 1)
                        if mine:
                            v.scalar_tensor_tensor(A.rearrange("p (w q) -> p w q", q=WQ),
                                                   B.rearrange("p (w q) -> p w q", q=WQ), 2.0, counts,
                                                   ALU.min, ALU.mult).then_inc(p_ready, 1)
                        else:
                            v.tensor_scalar(A, B, 2.0, None, ALU.min).then_inc(x_ready, 1)
                    elif mine:
                        dve.wait_ge(e_ready, dve_no(L, c, s) + 1)
                        A3 = A.rearrange("p (w q) -> p w q", q=WQ)
                        v.scalar_tensor_tensor(A3, A3, floor[:, s:s + 1], counts, ALU.max,
                                               ALU.mult).then_inc(p_ready, 1)
                    if not two_exps:
                        k0 = VEC_TOPS if first else 0
                        while k < T and (k - k0) * T // (T - k0) <= s:
                            top_step(L, c, k)
                            k += 1
                            if k == T:
                                join_tops(L, c)
                        if not first and s in CHAIN_AT:
                            maxima(L, c - 1, False, CHAIN_AT.index(s))
                        if s == ROW_AT and not last_chunk:
                            row_columns(L, c + 1, False, False)
                    if not first and s in Z_AT:
                        sums_inverse(L, c - 1, Z_AT.index(s))
                    if not first and L == 1:
                        if s == RESIDUAL_AT:
                            residual(c - 1)
                        if s == STATS[0]:
                            statistics(c - 1)
                        if s == STATS[1]:
                            aggregate()
                    if s == LEAD - 1 and two_exps:
                        rest_steps(L, c)

            def layer(L, two_exps):
                if not two_exps:
                    dve.wait_ge(fast_ready, L + 1)
                    row_columns(L, 0, True, False)
                for k in range(3, VEC_TOPS):
                    top_step(L, 0, k)
                chunk(L, 0, True, False, two_exps)
                with dve.Fori(1, NC - 1) as c:
                    chunk(L, c, False, False, two_exps)
                chunk(L, NC - 1, False, True, two_exps)
                if not two_exps:
                    for part in range(4):
                        maxima(L, NC - 1, False, part)

            for L in range(LAYERS):
                if L:
                    scalars(L)
                for k in range(3):
                    top_step(L, 0, k)
                    if L:
                        layer_vectors(L, k)
                dve.wait_ge(mode_ready, L + 1)
                dve.wait_ge(floor_ready, L + 1)
                with dve.If(dve.value_load(careful[0:1, 0:1], min_val=0, max_val=1)):
                    layer(L, True)
                with dve.Else():
                    layer(L, False)
                for part in range(3):
                    sums_inverse(L, NC - 1, part)
                if L == 1:
                    residual(NC - 1)
                    dve.wait_ge(raw_used, 2 * NC + 1)
                    dve.wait_ge(ln_ready, NC)
                    statistics(NC - 1)
                    dve.wait_ge(ln_lin, NC + 1)
                    aggregate()

        @block.scalar
        def _(act):
            a_ = nc.scalar
            for one in (raw_used, kappa_ready, *half_out, gen_out, gen_mm, gen_stored, rest_pe):
                act.sem_inc(one, 1)
            act.wait_ge(prep_T, 1)
            a_.activation(w1T[:, :, :], ps[:, PREP:PREP + KH * 128].rearrange("p (k f) -> p k f", k=KH), ACT.Copy)
            a_.activation(w2T[:, :, :], ps[:, PREP + 256:PREP + 512].rearrange("p (k f) -> p k f", k=KH), ACT.Copy)
            a_.activation(w3T[:, :], ps[:, PREP + 512:PREP + 640], ACT.Copy).then_inc(prep_sb, 1)
            act.wait_ge(prep_v, 1)
            a_.activation(w1v[:, :], ps[:, VEC:VEC + 2], ACT.Copy)
            for k in range(KH):
                a_.activation(w2[:, k, D:AW], ps[:, VEC + 2 + 2 * k:VEC + 4 + 2 * k], ACT.Copy)
            a_.activation(w3[:, D:AW], ps[:, VEC + 6:VEC + 8], ACT.Copy).then_inc(prep_done, 1)
            for i, (key, minus) in enumerate(((key_lo, 0.0), (key_col, -1.0))):
                act.wait_ge(keys_T, i + 1)
                for k in range(KC):
                    last = a_.activation(key[:, :, k].rearrange("p (g w) -> p g w", g=WG),
                                         tiles(KEYS[i] + 128 * WG * k, WG, rows=128), ACT.Copy, bias=minus)
                last.then_inc(keys_sb, 1)
            act.wait_ge(before_sum, 1)
            act.wait_ge(ln_ready, 1)
            for t in range(T):
                last = a_.activation(hA[:, t, 0:D], xr[:, t, :], ACT.Relu, bias=nbias[:, t:t + 1],
                                     scale=rstd[:, t:t + 1])
            last.then_inc(g0_ready, 1)
            def counts_out(t):
                for i, (w0, w1_, at_) in enumerate(HALF):
                    act.wait_ge(half_ok[i], t + 1)
                    a_.activation(C[:, bass.ds((t * TW + w0) * WC, (w1_ - w0) * WC)].rearrange(
                        "p (w c) -> p w c", c=WC), tiles(at_, w1_ - w0), ACT.Copy).then_inc(half_out[i], 1)

            for c in range(NC):
                with act.Fori(c * CT, (c + 1) * CT - 1) as t:
                    counts_out(t)
                act.wait_ge(g0_T, c + 1)
                if c:
                    act.wait_ge(ab0_ps, c)
                a_.activation(featT0[:, 0:4 * P].rearrange("p (t n) -> p t n", n=P), tiles(G0T[0], 4, rows=D), ACT.Copy)
                a_.activation(featT0[:, 4 * P:CT * P], ps[0:D, G0T[4]:G0T[4] + P], ACT.Copy).then_inc(g0_sb, 1)
                if c == NC - 1:
                    act.wait_ge(ab0_ps, NC)
                    a_.activation(ab[0][:, :, :], ps[0:P, AB0:AB0 + 2 * T].rearrange("p (t i) -> p t i", i=2),
                                  ACT.Copy).then_inc(ab_ready, 1)
                counts_out((c + 1) * CT - 1)

            def exps(A, B, a, al, out_sem):
                a_.activation(A.rearrange("p (t n) -> p t n", n=P), tiles(ROWU), ACT.Exp, bias=a)
                a_.activation(B.rearrange("p (t n) -> p t n", n=P), tiles(ROWV), ACT.Exp,
                              bias=al).then_inc(out_sem, 1)

            def rest_steps(L, c):
                act.wait_ge(flag_ok, 1)
                with act.If(act.value_load(general[0:1, 0:1], min_val=0, max_val=1)):
                    act.wait_ge(pe_done, step_no(L, c, LEAD))
                    with act.Fori(0, T) as s:
                        act.wait_ge(rest_pe, step_no(L, c, s) + 1)
                        one = bass.ds(s, 1)
                        exps(slot[LEAD - 1], top_b, ab[L][:, one, 0], a_leak[:, one], rest_e)

            def move_sums(L, c):
                n = L * NC + c
                act.wait_ge(pe_done, step_no(L, c, T))
                act.wait_ge(raw_used, n + 1)
                for i, (t0, t1) in enumerate(((0, 3), (3, CT))):
                    last = a_.activation(raw[:, t0:t1, :], acc3[i], ACT.Copy)
                last.then_inc(raw_ready, 1)

            def factors(L, c):
                act.wait_ge(back_ready, L * NC + c + 1)
                a_.activation(kappa[:, bass.ds(c * CT, CT)], back[:, :], ACT.Exp).then_inc(kappa_ready, 1)

            def copy_featT(L, c):
                act.wait_ge(feat_T, L * NC + c + 1)
                a_.activation(featT.rearrange("p (t n) -> p t n", n=P), tiles(WORK, rows=D),
                              ACT.Copy).then_inc(feat_sb, 1)

            def hidden(c):
                act.wait_ge(h1_ps, c + 1)
                for k in range(KH):
                    last = a_.activation(h1T[:, k, :].rearrange("p (t n) -> p t n", n=P),
                                         tiles(WORK + 128 * CT * k, rows=128), ACT.Relu, bias=b1c[:, k:k + 1])
                last.then_inc(h1_sb, 1)

            def new_features(L, c):
                act.wait_ge(new_ps, L * NC + c + 1)
                if L == 0:
                    act.wait_ge(ones_col, 1)
                for i, (t0, t1) in enumerate(((0, 3), (3, CT))):
                    tc = bass.ds(c * CT + t0, t1 - t0)
                    a_.activation(new_of[L][:, tc, 0:D], new3[i][:, :, 0:D], ACT.Copy)
                    last = a_.activation(ab[L + 1][:, tc, :], new3[i][:, :, D:AW], ACT.Copy)
                last.then_inc(new_sb, 1)

            def normalise(c):
                act.wait_ge(ln_ready, c + 2)
                act.wait_ge(feat_T, NC + c)
                for t in range(CT):
                    one = bass.ds(c * CT + t, 1)
                    last = a_.activation(gn[:, t, :], xr[:, one, :].rearrange("p o f -> p (o f)"), ACT.Relu,
                                         bias=nbias[:, t:t + 1], scale=rstd[:, t:t + 1])
                last.then_inc(g_ready, 1)

            def chunk(L, c, first, two_exps):
                for s in range(T):
                    if s == 0:
                        act.wait_ge(rows_ready, L * NC + c + 1)
                    if not two_exps and s + 1 in POOL_S:
                        if s + 1 > POOL_S[0] or L or not first:
                            act.wait_ge(x_ready, pool_no(L, c, s + 1))
                        a_.activation(side.rearrange("p (t n) -> p t n", n=P), tiles(ROWU), ACT.Relu,
                                      bias=to_relu[:, s + 1:s + 2]).then_inc(relu_done[L], 1)
                    n = step_no(L, c, s)
                    if two_exps:
                        if not (L == 0 and first and s < LEAD):
                            act.wait_ge(pe_done, n - (LEAD - 1))
                        if s or L or not first:
                            if s - 1 in POOL_S:
                                act.wait_ge(x_ready, pool_no(L, c, s))
                            else:
                                act.wait_ge(p_ready, dve_no(L, c, s))
                    elif not (L == 0 and first and (s < RING or s == T - 1)):
                        act.wait_ge(pe_done, n - RING if s < RING else n - (RING - 1) if s < T - 1 else n - (T - 1))
                    A = slot[s]
                    if two_exps:
                        exps(A, side, ab[L][:, s, 0:1], a_leak[:, s:s + 1],
                             e_pool[L] if s in POOL_S else e_ready)
                    elif s in POOL_S:
                        act.wait_ge(relu_done[L], pool_no(0, c, s) + 1)
                        a_.activation(A, side, ACT.Exp, bias=to_exp[:, s:s + 1]).then_inc(x_ready, 1)
                    else:
                        a_.activation(A.rearrange("p (t n) -> p t n", n=P), tiles(ROWU), ACT.Exp,
                                      bias=ab[L][:, s, 0:1]).then_inc(e_ready, 1)
                    if s == 0 and two_exps:
                        factors(L, c)
                    if s == KAPPA_AT and not two_exps and not first:
                        factors(L, c - 1)
                    if not first:
                        if s == SUMS_AT:
                            move_sums(L, c - 1)
                        if s == POST_ACT[L][0]:
                            if L == 1:
                                normalise(c - 1)
                            if L == 0:
                                copy_featT(L, c - 1)
                        if s == POST_ACT[L][1]:
                            if L == 0:
                                hidden(c - 1)
                            if L == 1:
                                copy_featT(L, c - 1)
                        if s == POST_ACT[L][2]:
                            new_features(L, c - 1)
                    if s == LEAD - 1 and two_exps:
                        rest_steps(L, c)

            def layer(L, two_exps):
                chunk(L, 0, True, two_exps)
                with act.Fori(1, NC) as c:
                    chunk(L, c, False, two_exps)
                move_sums(L, NC - 1)
                if not two_exps:
                    factors(L, NC - 1)

            for L in range(LAYERS):
                act.wait_ge(shift_ready, L + 1)
                a_.activation(floor[:, :], ab[L][:, :, 0], ACT.Exp, bias=shift[:, :],
                              scale=SLOPE).then_inc(floor_ready, 1)
                act.wait_ge(counts_done, 1)
                act.wait_ge(fast_ready, L + 1)
                act.wait_ge(mode_ready, L + 1)
                with act.If(act.value_load(careful[0:1, 0:1], min_val=0, max_val=1)):
                    layer(L, True)
                with act.Else():
                    layer(L, False)
                if L == 0:
                    copy_featT(L, NC - 1)
                    hidden(NC - 1)
                if L == 1:
                    normalise(NC - 1)
                    copy_featT(L, NC - 1)
                if L < 2:
                    new_features(L, NC - 1)
                    act.wait_ge(new_sb, (L + 1) * NC)
                    act.sem_inc(ab_ready, 1)

        @block.tensor
        def _(pe):
            mm, tr = nc.tensor.matmul, nc.tensor.transpose
            pe.wait_ge(dve_consts, 1)
            for k in range(NS):
                pe.wait_ge(before_ok, k + 1)
                for g in range(WG):
                    last = mm(ps[0:P, CNT + g:CNT + g + 1], before[:, k, P * g:P * (g + 1)], ones_b[:, :],
                              start=(k == 0 and g == 0), stop=(k == NS - 1), skip_group_check=True)
            last.then_inc(before_sum, 1)
            pe.wait_ge(weights_in, 16 * N_WEIGHTS)
            pe.wait_ge(consts, N_CONSTS)
            for k in range(KH):
                tr(ps[:, PREP + 128 * k:PREP + 128 * (k + 1)], w1[:, 128 * k:128 * (k + 1)], ident[:, :])
            for k in range(KH):
                tr(ps[:, PREP + 256 + 128 * k:PREP + 384 + 128 * k], w2[:, k, 0:D], ident[:, :])
            tr(ps[:, PREP + 512:PREP + 640], w3[:, 0:D], ident[:, :]).then_inc(prep_T, 1)
            pe.wait_ge(prep_sb, 1)
            for k in range(KH):
                mm(ps[:, VEC:VEC + 2], w1T[:, k, :], av1[:, k, :], start=(k == 0), stop=(k == KH - 1))
            for k in range(KH):
                mm(ps[:, VEC + 2 + 2 * k:VEC + 4 + 2 * k], w2T[:, k, :], av2[:, :], start=True, stop=True)
            mm(ps[:, VEC + 6:VEC + 8], w3T[:, :], av3[:, :], start=True, stop=True).then_inc(prep_v, 1)
            pe.wait_ge(prep_done, 1)
            for i, key in enumerate((k_lo, k_hi)):
                pe.wait_ge(keys_ok, i + 1)
                for k in range(KC):
                    for g in range(WG):
                        n = KEYS[i] + 128 * (WG * k + g)
                        last = tr(ps[0:128, n:n + P], key[:, g, 128 * k:128 * (k + 1)], ident[0:P, 0:P])
                last.then_inc(keys_T, 1)
            pe.wait_ge(keys_ok, 3)
            mm(ps[0:P, COV:COV + 1], ones_f[:, :], covered[:, :], start=True, stop=True).then_inc(covered_sum, 1)

            def count(t, i, by_halves=False):
                for j, (w0, w1_, at_) in enumerate(HALF):
                    if j == 0 or by_halves:
                        pe.wait_ge(hots_ok, t + 1 + j)
                    pe.wait_ge(half_out[j], t + 1)
                    for w in range(w0, w1_):
                        o = at_ + 128 * (w - w0)
                        for k in range(KC):
                            last = mm(ps[0:P, o:o + WC], hot_lo[i][:, :, KC * w + k], hot_col[i][:, :, KC * w + k],
                                      start=(k == 0), stop=(k == KC - 1))
                    last.then_inc(half_ok[j], 1)

            def attention_terms(c):
                for t in range(CT):
                    n = AB0 + 2 * (c * CT + t)
                    last = mm(ps[0:P, n:n + 2], featT0[:, P * t:P * (t + 1)], w1v[:, :], start=True, stop=True)
                last.then_inc(ab0_ps, 1)

            pe.wait_ge(keys_sb, 2)
            for c in range(NC):
                with pe.Fori(c * CT, (c + 1) * CT - 1, 2) as t:
                    count(t, c % 2)
                    count(t + 1, 1 - c % 2)
                pe.wait_ge(half_out[0], (c + 1) * CT)
                if c == 0:
                    pe.wait_ge(g0_ready, 1)
                    pe.wait_ge(flag_ok, 1)
                for t in range(CT):
                    last = tr(ps[0:D, G0T[t]:G0T[t] + P], hA[:, c * CT + t, 0:D], ident[0:P, 0:P])
                last.then_inc(g0_T, 1)
                pe.wait_ge(g0_sb, c + 1)
                attention_terms(c)
                if c == NC - 1:
                    pe.wait_ge(ab_ready, 1)
                count((c + 1) * CT - 1, c % 2, c == NC - 1)

            pe.wait_ge(flag_ok, 1)
            with pe.If(pe.value_load(general[0:1, 0:1], min_val=0, max_val=1)):
                HAND = EX // U
                pe.wait_ge(half_out[0], T + 1)
                pe.wait_ge(half_out[1], T + 1)
                with pe.Fori(0, P) as b:
                    pe.wait_ge(gen_out, b + 1)
                    mm(ps[0:P, 0:512], zeros[:, 0:P], zeros[:, 0:512], start=True, stop=False)
                    mm(ps[0:P, 512:512 + P], zeros[:, 0:P], zeros[:, 0:P], start=True, stop=False)
                    with pe.Fori(0, HAND) as i:
                        pe.wait_ge(gen_hots, b * HAND + i + 1)
                        for u in range(U):
                            for w in range(WQ):
                                last = mm(ps[0:P, 128 * w:128 * w + WC], g_hot[:, u, 0, :], g_hot[:, u, 1 + w, :],
                                          start=False, stop=False, skip_group_check=True)
                        last.then_inc(gen_mm, 1)
                    mm(ps[0:P, 0:512], zeros[:, 0:P], zeros[:, 0:512], start=False, stop=True)
                    mm(ps[0:P, 512:512 + P], zeros[:, 0:P], zeros[:, 0:P], start=False,
                       stop=True).then_inc(gen_sum, 1)

            def top_transpose(L, c, first):
                n = L * NC + c
                pe.wait_ge(top_done, (L * NC + c + 1) * (T + 1))
                if not (L == 0 and first):
                    pe.wait_ge(top_max, n)
                for t in range(CT):
                    last = tr(ps[0:P, WORK + 128 * t:WORK + 128 * t + P], top_a[:, P * t:P * (t + 1)],
                              ident[0:P, 0:P])
                last.then_inc(top_T, 1)

            def rows(L, c, first, two_exps):
                n = L * NC + c
                pe.wait_ge(uv_ready, n + 1)
                if not (L == 0 and first):
                    pe.wait_ge(e_ready, dve_no(L, c, 0))
                for i, at_ in enumerate((ROWU, ROWV) if two_exps else (ROWU,)):
                    for t in range(CT):
                        last = tr(ps[0:P, at_ + 128 * t:at_ + 128 * t + P],
                                  uv[:, i, t:t + 1].broadcast_to([P, P]), ident[0:P, 0:P])
                last.then_inc(rows_ready, 1)

            def products(L, A, feat, out_sem, last_of_group):
                for t in range(CT):
                    last = mm(ps[0:P, acc_at(t):acc_at(t) + HW], A[:, P * t:P * (t + 1)], feat,
                              start=False, stop=last_of_group, skip_group_check=last_of_group and t not in (2, CT - 1))
                last.then_inc(out_sem, 1)

            def rest_steps(L, c):
                with pe.If(pe.value_load(general[0:1, 0:1], min_val=0, max_val=1)):
                    with pe.Fori(0, T) as s:
                        pe.wait_ge(rest_p, step_no(L, c, s) + 1)
                        products(L, slot[LEAD - 1], h_of[L][:, bass.ds(s, 1), :].rearrange("p o f -> p (o f)"),
                                 rest_pe, False)

            def feat_transposes(L, c, source, ready, n, maxima_of):
                pe.wait_ge(ready, n)
                pe.wait_ge(top_max, L * NC + maxima_of + 1)
                for t in range(CT):
                    last = tr(ps[0:D, WORK + 128 * t:WORK + 128 * t + P], source[:, t, :], ident[0:P, 0:P])
                last.then_inc(feat_T, 1)

            def hidden(c):
                pe.wait_ge(feat_sb, c + 1)
                for k in range(KH):
                    for t in range(CT):
                        o = WORK + 128 * (CT * k + t)
                        last = mm(ps[:, o:o + P], w1[:, 128 * k:128 * (k + 1)], featT[:, P * t:P * (t + 1)],
                                  start=True, stop=True)
                last.then_inc(h1_ps, 1)

            def new_features(L, c):
                if L == 0:
                    pe.wait_ge(h1_sb, c + 1)
                else:
                    pe.wait_ge(feat_sb, NC + c + 1)
                for t in range(CT):
                    o = ps[0:P, new_at(t):new_at(t) + AW]
                    if L == 0:
                        for k in range(KH):
                            last = mm(o, h1T[:, k, P * t:P * (t + 1)], w2[:, k, :], start=(k == 0),
                                      stop=(k == KH - 1))
                    else:
                        last = mm(o, featT[:, P * t:P * (t + 1)], w3[:, :], start=True, stop=True)
                last.then_inc(new_ps, 1)

            def chunk(L, c, first, last_chunk, two_exps):
                if two_exps:
                    if not (L == 0 and first):
                        pe.wait_ge(e_ready, dve_no(L, c, 0))
                    top_transpose(L, c, first)
                    rows(L, c, first, True)
                if not (L == 0 and first):
                    pe.wait_ge(raw_ready, L * NC + c)
                for at_, n in ((0, 3 * HW), (512, 2 * HW)):
                    mm(ps[0:P, at_:at_ + n], zeros[:, 0:P], zeros[:, 0:n], start=True, stop=False)
                for s in range(T):
                    if s in POOL_S:
                        pe.wait_ge(q_ready, pool_no(L, c, s) + 1)
                    else:
                        pe.wait_ge(p_ready, dve_no(L, c, s) + 1)
                    products(L, slot[s], h_of[L][:, s, :], pe_done, s == T - 1)
                    if s == LEAD - 1 and two_exps:
                        rest_steps(L, c)
                    if not first:
                        if L == 0 and s == POST_PE[L][0]:
                            feat_transposes(L, c - 1, agg, raw_used, c + 1, c if two_exps else c - 1)
                        if L == 0 and s == POST_PE[L][1]:
                            hidden(c - 1)
                        if L == 1 and s == POST_PE[L][0]:
                            feat_transposes(L, c - 1, gn, g_ready, c, c if two_exps else c - 1)
                        if L < 2 and s == POST_PE[L][2]:
                            new_features(L, c - 1)
                    if s == ROWS_PE and not last_chunk and not two_exps:
                        rows(L, c + 1, False, False)
                    if not two_exps and s == T - 1:
                        if L < 2 and not first:
                            pe.wait_ge(new_sb, L * NC + c)
                        top_transpose(L, c, first)

            def layer(L, two_exps):
                if not two_exps:
                    rows(L, 0, True, False)
                chunk(L, 0, True, False, two_exps)
                with pe.Fori(1, NC - 1) as c:
                    chunk(L, c, False, False, two_exps)
                chunk(L, NC - 1, False, True, two_exps)

            for L in range(LAYERS):
                if L:
                    pe.wait_ge(new_sb, L * NC)
                else:
                    pe.wait_ge(half_out[0], T + 1)
                    pe.wait_ge(half_out[1], T + 1)
                    pe.wait_ge(counts_done, 1)
                pe.wait_ge(mode_ready, L + 1)
                with pe.If(pe.value_load(careful[0:1, 0:1], min_val=0, max_val=1)):
                    layer(L, True)
                with pe.Else():
                    layer(L, False)
                if L == 0:
                    feat_transposes(L, NC - 1, agg, raw_used, NC + 1, NC - 1)
                    hidden(NC - 1)
                if L == 1:
                    feat_transposes(L, NC - 1, gn, g_ready, NC, NC - 1)
                if L < 2:
                    new_features(L, NC - 1)


def kernel(**inputs):
    import numpy as np
    import concourse.bacc as bacc
    from concourse import mybir as mb
    from concourse.bass_utils import run_bass_kernel_spmd

    arrays = {
        "x": inputs["x"],
        "edges": np.stack([inputs["src"], inputs["dst"]], axis=1),
        "W1": inputs["L0_gnn_W1"], "a_src1": inputs["L0_gnn_a_src1"], "a_dst1": inputs["L0_gnn_a_dst1"],
        "b1": inputs["L0_gnn_b1"],
        "W2": inputs["L0_gnn_W2"], "a_src2": inputs["L0_gnn_a_src2"], "a_dst2": inputs["L0_gnn_a_dst2"],
        "b2": inputs["L0_gnn_b2"],
        "W3": inputs["L1_gnn_W"], "a_src3": inputs["L1_gnn_att_src"], "a_dst3": inputs["L1_gnn_att_dst"],
        "b3": inputs["L1_gnn_bias"],
    }
    arrays = {n: np.ascontiguousarray(a) for n, a in arrays.items()}
    nc = bacc.Bacc("TRN2", target_bir_lowering=False, num_devices=1)
    aps = {n: nc.dram_tensor("in_" + n, a.shape, mb.dt.from_np(a.dtype), kind="ExternalInput").ap()
           for n, a in arrays.items()}
    out = nc.dram_tensor("out", inputs["x"].shape, mb.dt.float32, kind="ExternalOutput").ap()
    gat_stack_kernel(nc, out=out, **aps)
    r = run_bass_kernel_spmd(nc, [{"in_" + n: a for n, a in arrays.items()}], core_ids=[0])
    return r.results[0]["out"]
```
